# Optimizing a Trainium2 kernel written in Bass

```python
import numpy as np
import jax
import jax.numpy as jnp

def _softmax(x, axis=-1):
    return jax.nn.softmax(x, axis=axis)

def _gelu(x):
    return jax.nn.gelu(x, approximate=True)

def _silu(x):
    return jax.nn.silu(x)

def _sigmoid(x):
    return jax.nn.sigmoid(x)

def _layernorm(x, axis=-1, eps=1e-05):
    m = jnp.mean(x, axis=axis, keepdims=True)
    v = jnp.var(x, axis=axis, keepdims=True)
    return (x - m) / jnp.sqrt(v + eps)

def _scatter_add(tgt, idx, src, axis=0):
    return tgt.at[idx].add(src)

def _segment_sum(src, seg, n):
    return jax.ops.segment_sum(src, seg, n)
kernel_name = 'mk_vit_tower_cls_d1_tok_img512_r4_650008'

def setup_inputs(seed: int=0):
    np.random.seed(seed)
    _w = jnp.asarray

    def _rec_inputs():
        import jax
        import jax.numpy as jnp
        _rk = jax.random.key(seed)
        x = -0.000356955 + 1 * jax.random.normal(jax.random.fold_in(_rk, 1), (64, 3, 224, 224), jnp.float32)
        cls_tok = 0.02 * jax.random.normal(jax.random.fold_in(_rk, 5), (1, 1, 128), jnp.float32)
        return (x, cls_tok)
    x, cls_tok = _rec_inputs()

    def _L0_tok_setup():
        import jax, jax.numpy as jnp
        import numpy as np
        P = 16
        SHIFT = P // 2
        EPS = 1e-05

        def _shift2d(img, dy, dx):
            H, W = (img.shape[2], img.shape[3])
            pad = ((0, 0), (0, 0), (max(dy, 0), max(-dy, 0)), (max(dx, 0), max(-dx, 0)))
            z = jnp.pad(img, pad)
            return z[:, :, max(-dy, 0):max(-dy, 0) + H, max(-dx, 0):max(-dx, 0) + W]

        def _patchify(img):
            B, C, H, W = img.shape
            nH, nW = (H // P, W // P)
            t = img.reshape(B, C, nH, P, nW, P).transpose(0, 2, 4, 1, 3, 5)
            return t.reshape(B, nH * nW, C * P * P)
        key = jax.random.key(seed)
        ks = jax.random.split(key, 8)
        B, C, H, Wd = (128, 3, 224, 224)
        embed_dim = 128
        d_main = embed_dim // 2
        d_shift = embed_dim // 8
        fan_in = C * P * P
        std = 0.02
        x = jax.random.normal(ks[0], (B, C, H, Wd), dtype=jnp.float32)
        W_main = jax.random.normal(ks[1], (d_main, fan_in), dtype=jnp.float32) * std
        b_main = jnp.zeros((d_main,), dtype=jnp.float32)
        W_sx = jax.random.normal(ks[2], (d_shift, fan_in), dtype=jnp.float32) * std
        b_sx = jnp.zeros((d_shift,), dtype=jnp.float32)
        W_sy = jax.random.normal(ks[3], (d_shift, fan_in), dtype=jnp.float32) * std
        b_sy = jnp.zeros((d_shift,), dtype=jnp.float32)
        ln_g = jnp.ones((embed_dim,), dtype=jnp.float32)
        ln_b = jnp.zeros((embed_dim,), dtype=jnp.float32)
        return {'x': x, 'W_main': W_main, 'b_main': b_main, 'W_sx': W_sx, 'b_sx': b_sx, 'W_sy': W_sy, 'b_sy': b_sy, 'ln_g': ln_g, 'ln_b': ln_b}
    _L0_tok_all = _L0_tok_setup()
    _L0_tok_in = {k: v for k, v in _L0_tok_all.items() if k in ('W_main', 'b_main', 'W_sx', 'b_sx', 'W_sy', 'b_sy', 'ln_g', 'ln_b')}
    del _L0_tok_all

    def _L0_attn_setup():
        import jax, jax.numpy as jnp
        import numpy as np
        DIM = 128
        NUM_HEADS = 8
        HEAD_DIM = DIM // NUM_HEADS
        SCALE = HEAD_DIM ** (-0.5)
        key = jax.random.key(seed)
        k_x, k_qkv, k_proj, k_pb = jax.random.split(key, 4)
        x = jax.random.normal(k_x, (2, 1024, DIM), dtype=jnp.float32)
        w_qkv = jax.random.normal(k_qkv, (3 * DIM, DIM), dtype=jnp.float32) * DIM ** (-0.5)
        w_proj = jax.random.normal(k_proj, (DIM, DIM), dtype=jnp.float32) * DIM ** (-0.5)
        b_proj = jax.random.normal(k_pb, (DIM,), dtype=jnp.float32) * 0.01
        return {'x': x, 'w_qkv': w_qkv, 'w_proj': w_proj, 'b_proj': b_proj}
    _L0_attn_all = _L0_attn_setup()
    _L0_attn_in = {k: v for k, v in _L0_attn_all.items() if k in ('w_qkv', 'w_proj', 'b_proj')}
    del _L0_attn_all

    def _L0_ffn_setup():
        import jax, jax.numpy as jnp
        import numpy as np
        TOP_K = 6
        CAP_FACTOR = 2.0
        key = jax.random.key(seed)
        ks = jax.random.split(key, 9)
        B, S, D, F, E, SH = (4, 512, 128, 64, 64, 2)
        return {'x': jax.random.normal(ks[0], (B, S, D), jnp.float32), 'router_w': jax.random.normal(ks[1], (E, D), jnp.float32) * 0.02, 'bias': jnp.zeros((E,), jnp.float32), 'shared_w_gate': jax.random.normal(ks[2], (SH, F, D), jnp.float32) * 0.02, 'shared_w_up': jax.random.normal(ks[3], (SH, F, D), jnp.float32) * 0.02, 'shared_w_down': jax.random.normal(ks[4], (SH, D, F), jnp.float32) * 0.02, 'w_gate': jax.random.normal(ks[5], (E, F, D), jnp.float32) * 0.02, 'w_up': jax.random.normal(ks[6], (E, F, D), jnp.float32) * 0.02, 'w_down': jax.random.normal(ks[7], (E, D, F), jnp.float32) * 0.02}
    _L0_ffn_all = _L0_ffn_setup()
    _L0_ffn_in = {k: v for k, v in _L0_ffn_all.items() if k in ('router_w', 'bias', 'shared_w_gate', 'shared_w_up', 'shared_w_down', 'w_gate', 'w_up', 'w_down')}
    del _L0_ffn_all
    return {'x': x, 'cls_tok': cls_tok, 'L0_tok_W_main': _L0_tok_in['W_main'], 'L0_tok_b_main': _L0_tok_in['b_main'], 'L0_tok_W_sx': _L0_tok_in['W_sx'], 'L0_tok_b_sx': _L0_tok_in['b_sx'], 'L0_tok_W_sy': _L0_tok_in['W_sy'], 'L0_tok_b_sy': _L0_tok_in['b_sy'], 'L0_tok_ln_g': _L0_tok_in['ln_g'], 'L0_tok_ln_b': _L0_tok_in['ln_b'], 'L0_attn_w_qkv': _L0_attn_in['w_qkv'], 'L0_attn_w_proj': _L0_attn_in['w_proj'], 'L0_attn_b_proj': _L0_attn_in['b_proj'], 'L0_ffn_router_w': _L0_ffn_in['router_w'], 'L0_ffn_bias': _L0_ffn_in['bias'], 'L0_ffn_shared_w_gate': _L0_ffn_in['shared_w_gate'], 'L0_ffn_shared_w_up': _L0_ffn_in['shared_w_up'], 'L0_ffn_shared_w_down': _L0_ffn_in['shared_w_down'], 'L0_ffn_w_gate': _L0_ffn_in['w_gate'], 'L0_ffn_w_up': _L0_ffn_in['w_up'], 'L0_ffn_w_down': _L0_ffn_in['w_down']}

def reference(x, cls_tok, L0_tok_W_main, L0_tok_b_main, L0_tok_W_sx, L0_tok_b_sx, L0_tok_W_sy, L0_tok_b_sy, L0_tok_ln_g, L0_tok_ln_b, L0_attn_w_qkv, L0_attn_w_proj, L0_attn_b_proj, L0_ffn_router_w, L0_ffn_bias, L0_ffn_shared_w_gate, L0_ffn_shared_w_up, L0_ffn_shared_w_down, L0_ffn_w_gate, L0_ffn_w_up, L0_ffn_w_down):
    import jax
    import jax.numpy as jnp

    def _L0_tok_ref(x, W_main, b_main, W_sx, b_sx, W_sy, b_sy, ln_g, ln_b):
        import jax, jax.numpy as jnp
        import numpy as np
        P = 16
        SHIFT = P // 2
        EPS = 1e-05

        def _shift2d(img, dy, dx):
            H, W = (img.shape[2], img.shape[3])
            pad = ((0, 0), (0, 0), (max(dy, 0), max(-dy, 0)), (max(dx, 0), max(-dx, 0)))
            z = jnp.pad(img, pad)
            return z[:, :, max(-dy, 0):max(-dy, 0) + H, max(-dx, 0):max(-dx, 0) + W]

        def _patchify(img):
            B, C, H, W = img.shape
            nH, nW = (H // P, W // P)
            t = img.reshape(B, C, nH, P, nW, P).transpose(0, 2, 4, 1, 3, 5)
            return t.reshape(B, nH * nW, C * P * P)

        def proj(img, W, b):
            return jnp.einsum('bnf,of->bno', _patchify(img), W) + b
        main = proj(x, W_main, b_main)
        xl = proj(_shift2d(x, 0, -SHIFT), W_sx, b_sx)
        xr = proj(_shift2d(x, 0, SHIFT), W_sx, b_sx)
        yu = proj(_shift2d(x, -SHIFT, 0), W_sy, b_sy)
        yd = proj(_shift2d(x, SHIFT, 0), W_sy, b_sy)
        tok = jnp.concatenate([main, xl, xr, yu, yd], axis=-1)
        mu = jnp.mean(tok, axis=-1, keepdims=True)
        var = jnp.mean(jnp.square(tok - mu), axis=-1, keepdims=True)
        return (tok - mu) * jax.lax.rsqrt(var + EPS) * ln_g + ln_b

    def _L0_attn_ref(x, w_qkv, w_proj, b_proj):
        import jax, jax.numpy as jnp
        import numpy as np
        DIM = 128
        NUM_HEADS = 8
        HEAD_DIM = DIM // NUM_HEADS
        SCALE = HEAD_DIM ** (-0.5)
        B, N, D = x.shape
        H, Hd = (NUM_HEADS, HEAD_DIM)
        qkv = (x @ w_qkv.T).reshape(B, N, 3, H, Hd).transpose(2, 0, 3, 1, 4)
        q, k, v = (qkv[0], qkv[1], qkv[2])
        attn = jnp.einsum('bhqd,bhkd->bhqk', q, k) * SCALE
        attn = jax.nn.softmax(attn, axis=-1)
        out = jnp.einsum('bhqk,bhkd->bhqd', attn, v)
        out = out.transpose(0, 2, 1, 3).reshape(B, N, D)
        return out @ w_proj.T + b_proj

    def _L0_ffn_ref(x, router_w, bias, shared_w_gate, shared_w_up, shared_w_down, w_gate, w_up, w_down):
        import jax, jax.numpy as jnp
        import numpy as np
        TOP_K = 6
        CAP_FACTOR = 2.0
        B, S, D = x.shape
        E = router_w.shape[0]
        K = TOP_K
        N = B * S
        C = max(1, int(N * K * CAP_FACTOR / E))
        router_logits = jnp.einsum('bsd,ed->bse', x, router_w) + bias
        hg = jnp.einsum('bsd,efd->bsef', x, shared_w_gate)
        hu = jnp.einsum('bsd,efd->bsef', x, shared_w_up)
        shared_out = jnp.einsum('bsef,edf->bsd', jax.nn.silu(hg) * hu, shared_w_down)
        shared_out = shared_out / shared_w_gate.shape[0]
        router_probs = jax.nn.softmax(router_logits, axis=-1)
        topk_p, topk_i = jax.lax.top_k(router_probs, K)
        topk_p = topk_p / (jnp.sum(topk_p, axis=-1, keepdims=True) + 1e-09)
        x_flat = x.reshape(N, D)
        flat_e = topk_i.reshape(-1)
        flat_g = topk_p.reshape(-1)
        token_ids = jnp.repeat(jnp.arange(N), K)
        order = jnp.argsort(flat_e)
        se = flat_e[order]
        st = token_ids[order]
        sg = flat_g[order]
        M = se.shape[0]
        pos = jnp.arange(M)
        is_first = jnp.concatenate([jnp.ones((1,), bool), se[1:] != se[:-1]])
        group_starts = jax.lax.cummax(pos * is_first.astype(pos.dtype))
        slot = pos - group_starts
        valid = slot < C
        safe_slot = jnp.where(valid, slot, C)
        expert_in = jnp.zeros((E, C + 1, D), x.dtype).at[se, safe_slot].set(x_flat[st])
        expert_gate = jnp.zeros((E, C + 1), x.dtype).at[se, safe_slot].set(sg)
        expert_tok = jnp.full((E, C + 1), N, jnp.int32).at[se, safe_slot].set(st.astype(jnp.int32))
        expert_mask = jnp.zeros((E, C + 1), bool).at[se, safe_slot].set(valid)
        expert_in = expert_in[:, :C]
        expert_gate = expert_gate[:, :C]
        expert_tok = expert_tok[:, :C]
        expert_mask = expert_mask[:, :C]
        hg = jnp.einsum('ecd,efd->ecf', expert_in, w_gate)
        hu = jnp.einsum('ecd,efd->ecf', expert_in, w_up)
        expert_out = jnp.einsum('ecf,edf->ecd', jax.nn.silu(hg) * hu, w_down)
        fm = expert_mask.reshape(-1)
        dst = jnp.where(fm, expert_tok.reshape(-1), N)
        fg = jnp.where(fm, expert_gate.reshape(-1), jnp.zeros((), x.dtype))
        sparse = jax.ops.segment_sum(fg[:, None] * expert_out.reshape(-1, D), dst, num_segments=N + 1)[:N]
        return shared_out + sparse.reshape(B, S, D)
    h = _L0_tok_ref(x, L0_tok_W_main, L0_tok_b_main, L0_tok_W_sx, L0_tok_b_sx, L0_tok_W_sy, L0_tok_b_sy, L0_tok_ln_g, L0_tok_ln_b)
    h = jnp.concatenate([jnp.broadcast_to(cls_tok, (h.shape[0], 1, h.shape[2])), h], axis=1)
    h = h + _L0_attn_ref(_layernorm(h, axis=-1), L0_attn_w_qkv, L0_attn_w_proj, L0_attn_b_proj)
    h = h + _L0_ffn_ref(_layernorm(h, axis=-1), L0_ffn_router_w, L0_ffn_bias, L0_ffn_shared_w_gate, L0_ffn_shared_w_up, L0_ffn_shared_w_down, L0_ffn_w_gate, L0_ffn_w_up, L0_ffn_w_down)
    return h

_drawn_inputs = setup_inputs


def setup_inputs(seed=0):
    import zlib

    import numpy as np

    out = dict(_drawn_inputs(seed))
    spreads = {'L0_tok_b_main': (0.0, 0.1),
     'L0_tok_b_sx': (0.0, 0.1),
     'L0_tok_b_sy': (0.0, 0.1),
     'L0_tok_ln_g': (1.0, 0.2),
     'L0_tok_ln_b': (0.0, 0.1),
     'L0_ffn_bias': (0.0, 0.8)}
    factors = {'cls_tok': 3.266,
     'L0_attn_b_proj': 5.948,
     'L0_ffn_router_w': 8.0,
     'L0_ffn_shared_w_gate': 8.0,
     'L0_ffn_shared_w_up': 8.0,
     'L0_ffn_shared_w_down': 8.0,
     'L0_ffn_w_gate': 8.0,
     'L0_ffn_w_up': 8.0,
     'L0_ffn_w_down': 8.0}
    for name, (base, spread) in spreads.items():
        noise = np.random.default_rng([zlib.crc32(name.encode()), seed]).standard_normal(out[name].shape)
        drawn = base * np.exp(spread * noise) if base else spread * noise
        out[name] = jnp.asarray(drawn.astype(out[name].dtype))
    for name, factor in factors.items():
        out[name] = (out[name] * factor).astype(out[name].dtype)
    return out
```

```python
from contextlib import ExitStack

import concourse.bass as bass
from concourse import mybir

F32 = mybir.dt.float32
F32R = mybir.dt.float32r
BF16 = mybir.dt.bfloat16
ALU = mybir.AluOpType
ACT = mybir.ActivationFunctionType
AX_X = mybir.AxisListType.X

D = 128
HEADS, HD = 8, 16
PS, HP = 16, 8
GRID = 14
NTOK = 1 + GRID * GRID
PAIR = 2 * NTOK
COLS = PAIR + 2
T = 99
START = [0, T, NTOK, NTOK + T]
WIDTH = [T, NTOK - T, T, NTOK - T]
EXPERTS, TOPK, F = 64, 6, 64
ROUTED = EXPERTS // 2
UNITS = ROUTED + 1
EPS = 1e-5
GATE_EPS = 1e-9
LOWEST = -104.0
FILLER = -1e30
CHOSEN = 1.0
CREDITS_Y = 2
ROUTE_STEPS = 7


def vit_layer(nc, x, conv_w, conv_b, masks, perm, ident, cls_tok, ln_g, ln_b, w_qk, w_v, w_p, b_proj,
              w_r, b_r, w_gate, w_up, w_down, select, before, out):
    B = x.shape[0]
    PAIRS = B // 2
    CAPACITY = float(max(1, int(B * NTOK * TOPK * 2.0 / EXPERTS)))

    with ExitStack() as ctx:
        def sb(name, shape, dt=F32):
            return ctx.enter_context(nc.sbuf_tensor(name, shape, dt))

        def sem(name):
            return ctx.enter_context(nc.semaphore(name))

        def sems(name, n):
            return [sem(f"{name}{i}") for i in range(n)]

        gate_ps = ctx.enter_context(nc.psum_tensor("gate_ps", [128, 512], F32))
        up_ps = ctx.enter_context(nc.psum_tensor("up_ps", [128, 512], F32))
        share_ps = ctx.enter_context(nc.psum_tensor("share_ps", [128, 512], F32))
        y_ps = ctx.enter_context(nc.psum_tensor("y_ps", [128, 512], F32))
        A = ctx.enter_context(nc.psum_tensor("A", [128, 4, 512], F32))
        SCORES = A[0:T, 0:2, 0:PAIR].rearrange("p a (h k) -> p a h k", h=2)

        conv_sb = sb("conv_sb", [96, HP, 128])
        conv_bias = sb("conv_bias", [128, 1])
        mask_sb = sb("mask_sb", [128, 2])
        perm_sb = sb("perm_sb", [128, 128])
        id_sb = sb("id_sb", [128, 128])
        cls_sb = sb("cls_sb", [1, 128])
        lng_sb = sb("lng_sb", [T, 128])
        lnb_sb = sb("lnb_sb", [T, 128])
        bproj_sb = sb("bproj_sb", [T, 128])
        brout_sb = sb("brout_sb", [T, EXPERTS])
        wqk_sb = sb("wqk_sb", [128, 4, 128])
        wv_sb = sb("wv_sb", [128, 128])
        wp_sb = sb("wp_sb", [128, 2, 128])
        wr_sb = sb("wr_sb", [128, EXPERTS])
        before_sb = sb("before_sb", [T, 2, T], BF16)
        half_neg = sb("half_neg", [T, 4])
        gate_hi = sb("gate_hi", [128, UNITS, 128], F32R)
        gate_lo = sb("gate_lo", [128, UNITS, 128], F32R)
        up_hi = sb("up_hi", [128, UNITS, 128], F32R)
        up_lo = sb("up_lo", [128, UNITS, 128], F32R)
        down_sb = sb("down_sb", [128, UNITS, 128])
        stage = down_sb[:].rearrange("p u m -> p (u m)")
        select_sb = sb("select_sb", [128, ROUTED, 128], F32R)

        image = sb("image", [96, 2 * GRID, GRID * PS])
        raw = sb("raw", [128, COLS])
        pad_y = sb("pad_y", [128, 2, 16, 16])
        pad_x = sb("pad_x", [128, 2, 16, 16])
        bn = sb("bn", [T, 3, 4, 6])
        mv = sb("mv", [T, 3, 4, 2])
        var_eps = sb("var_eps", [T, 3, 4])
        rstd = sb("rstd", [T, 3, 4])
        h0 = sb("h0", [T, 4, 128])
        xn = sb("xn", [T, 4, 128])
        xT1 = sb("xT1", [128, COLS])
        q_sb = sb("q_sb", [128, 2, COLS])
        k_sb = sb("k_sb", [128, 2, 4, PAIR])
        v_sb = sb("v_sb", [T, 4, HEADS, 32])
        negmax = sb("negmax", [T, 8, 4])
        sums = sb("sums", [T, 4, HEADS])
        rinv = sb("rinv", [T, 4, HEADS])
        out_sb = sb("out_sb", [T, 4, 128])
        rwide = [xn, out_sb]
        prob = sb("prob", [T, 4, NTOK + 1])
        probT = sb("probT", [T, 2, 2, 4, T])
        heads = sb("heads", [128, 2, COLS])
        h1 = sb("h1", [T, 4, 128])
        before_f = h1[:].rearrange("p j d -> p (j d)")[:, 0:2 * T].rearrange("p (a b) -> p a b", a=2)
        resid = sb("resid", [T, 4, 128])
        xT2 = sb("xT2", [128, COLS])
        logit = sb("logit", [T, 4, EXPERTS])
        lmax = sb("lmax", [T, 4])
        shifted = sb("shifted", [T, 4, EXPERTS + 2])
        marked = sb("marked", [T, 4, EXPERTS + 2])
        top8 = sb("top8", [T, 4, 8])
        topr = sb("topr", [T, 4, 8])
        chosen = sb("chosen", [T, 4, EXPERTS], BF16)
        expl = sb("expl", [T, 4, EXPERTS])
        expc = expl
        zsum = sb("zsum", [T, 3, 4])
        rden = sb("rden", [T, 4])
        slot = logit
        kept = marked[:, :, 0:EXPERTS]
        counts = sb("counts", [T, EXPERTS])
        share_tok = sb("share_tok", [T, 4, 128], F32R)
        share_sb = sb("share_sb", [128, PAIR], F32R)
        x_hi = sb("x_hi", [128, PAIR], F32R)
        x_lo = sb("x_lo", [128, PAIR], F32R)
        silu = sb("silu", [128, 2, PAIR])
        hidden = sb("hidden", [128, 3, PAIR])
        y_sb = raw

        consts_in = sem("consts_in")
        weights_in = sem("weights_in")
        stage_in = sem("stage_in")
        split_step = sem("split_step")
        presets = sem("presets")
        image_in = sem("image_in")
        conv_done = sem("conv_done")
        conv_read = sem("conv_read")
        raw_step = sem("raw_step")
        raw_ready = sem("raw_ready")
        raw_t = sem("raw_t")
        bn_done = sems("bn_done", 3)
        var_ready = sems("var_ready", 3)
        eps_added = sems("eps_added", 3)
        rstd_ready = sems("rstd_ready", 3)
        z_ready = sem("z_ready")
        scaled = sem("scaled")
        shifted_h0 = sem("shifted_h0")
        h0_ready = sem("h0_ready")
        h0_biased = sem("h0_biased")
        xn1_ready = sem("xn1_ready")
        xn1_t = sem("xn1_t")
        xT1_ready = sem("xT1_ready")
        qk_done = sems("qk_done", 4)
        qk_ready = sems("qk_ready", 4)
        v_done = sem("v_done")
        v_ready = sem("v_ready")
        scores_done = sems("scores_done", 8)
        max_ready = sems("max_ready", 8)
        exp_done = sems("exp_done", 8)
        pt_done = [sems("pt_done_a", 8), sems("pt_done_b", 8)]
        pt_ready = [sems("pt_ready_a", 8), sems("pt_ready_b", 8)]
        pv_done = sems("pv_done", 8)
        pv_read = sems("pv_read", 8)
        rinv_done = sem("rinv_done")
        rwide_ready = sem("rwide_ready")
        rwide_t = sem("rwide_t")
        heads_ready = sem("heads_ready")
        proj_done = sem("proj_done")
        h1_ready = sem("h1_ready")
        xn2_ready = sem("xn2_ready")
        xn2_t = sem("xn2_t")
        xT2_ready = sem("xT2_ready")
        logits_done = sem("logits_done")
        route_step = sem("route_step")
        shifted_ready = sem("shifted_ready")
        chosen_ready = sem("chosen_ready")
        expl_ready = sem("expl_ready")
        expc_ready = sem("expc_ready")
        zsum_ready = sem("zsum_ready")
        den_ready = sem("den_ready")
        rden_ready = sem("rden_ready")
        rank_done = sem("rank_done")
        slot_ready = sem("slot_ready")
        kept_ready = sem("kept_ready")
        share_ready = sem("share_ready")
        share_hi = sem("share_hi")
        share_tok_ready = sem("share_tok_ready")
        share_t = sem("share_t")
        share_sb_ready = sem("share_sb_ready")
        x_hi_ready = sem("x_hi_ready")
        x_lo_ready = sem("x_lo_ready")
        resid_copied = sem("resid_copied")
        gate_done = sem("gate_done")
        up_done = sem("up_done")
        share_done = sem("share_done")
        silu_done = sem("silu_done")
        gated_done = sem("gated_done")
        hidden_done = sem("hidden_done")
        y_done = sem("y_done")
        y_read = sem("y_read")
        y_t = sem("y_t")
        out_added = sem("out_added")
        out_stored = sem("out_stored")
        out_free = sem("out_free")

        NCONST = 17
        x_view = x.rearrange("(p b) c (t y) x -> p c y b t x", b=2, y=PS)
        out_view = out.rearrange("(p b) t d -> p t b d", b=2)
        IMAGE = 12 * 16
        STORED = 2 * 16

        def combo(c):
            return c // 4, c // 2 % 2, c % 2

        def hold(eng, sem_, value):
            eng.wait_ge(sem_, value)
            eng.nop(nofuse=True)

        block = ctx.enter_context(nc.Block())

        @block.sync
        def _(sp):
            for dst, src in ((conv_sb[:], conv_w.rearrange("p (a b) -> p a b", a=HP)),
                             (conv_bias[:], conv_b), (mask_sb[:], masks), (perm_sb[:], perm),
                             (id_sb[:], ident), (cls_sb[:], cls_tok),
                             (wqk_sb[:], w_qk.rearrange("p (a b) -> p a b", a=4)), (wv_sb[:], w_v),
                             (wp_sb[:], w_p.rearrange("p (a b) -> p a b", a=2)), (wr_sb[:], w_r),
                             (before_f, before.rearrange("p (a b) -> p a b", a=2))):
                sp.dma_start(dst, src).then_inc(consts_in, 16)

            def load_image(p):
                for g in range(2):
                    w = GRID * PS - HP * g
                    for c in range(3):
                        for b in range(2):
                            sp.dma_start(image[48 * g + 16 * c:48 * g + 16 * c + 16, GRID * b:GRID * (b + 1), 0:w],
                                         x_view[p, c, :, b, :, HP * g:HP * g + w]).then_inc(image_in, 16)

            load_image(0)
            for dst, src in ((lng_sb, ln_g), (lnb_sb, ln_b), (bproj_sb, b_proj), (brout_sb, b_r)):
                sp.dma_start(dst[:], src).then_inc(consts_in, 16)
            sp.dma_start(stage, w_gate).then_inc(stage_in, 16)
            sp.wait_ge(split_step, 2)
            sp.dma_start(stage, w_up).then_inc(stage_in, 16)
            sp.wait_ge(split_step, 4)
            sp.dma_start(stage[:, 0:ROUTED * 128], select).then_inc(stage_in, 16)
            sp.wait_ge(split_step, 5)
            sp.dma_start(stage, w_down).then_inc(weights_in, 16)
            sp.wait_ge(conv_done, 1)
            load_image(1)

            def store(p):
                sp.wait_ge(out_added, p + 1 + CREDITS_Y)
                for half in range(2):
                    w = WIDTH[half]
                    sp.dma_start(out_view[p, T * half:T * half + w],
                                 out_sb[0:w].rearrange("t (b h) d -> t h b d", h=2)[:, half]
                                 ).then_inc(out_stored, 16)
                sp.wait_ge(out_stored, STORED * (p + 1))
                sp.sem_inc(out_free, 1)

            with sp.Fori(0, PAIRS - 2) as p:
                sp.wait_ge(conv_done, p + 2)
                load_image(p + 2)
                store(p)
            store(PAIRS - 2)
            store(PAIRS - 1)

        @block.tensor
        def _(pe):
            mm, tr = nc.tensor.matmul, nc.tensor.transpose
            ident_t = id_sb[0:T, 0:T]

            def conv(lo, hi):
                for px in range(lo, hi):
                    last = mm(A[:, 0, 0:2 * GRID * GRID].rearrange("p (t x) -> p t x", x=GRID),
                              conv_sb[:, px, :],
                              image[:].rearrange("p t (x q) -> p t x q", q=PS)[:, :, :, px],
                              start=(px == 0), stop=(px == HP - 1))
                return last

            def tokens_to_features(dst, src):
                for j in range(4):
                    w = WIDTH[j]
                    last = tr(dst[:, START[j]:START[j] + w], src[0:w, j, :], id_sb[0:w, 0:w])
                return last

            def scores(c):
                b, g, half = combo(c)
                j = 2 * b + half
                for r in range(4):
                    last = mm(SCORES[:, r // 2, r % 2], q_sb[:, g, START[j]:START[j] + T],
                              k_sb[:, g, r, NTOK * b:NTOK * (b + 1)], start=True, stop=True)
                last.then_inc(scores_done[c], 1)

            def transpose_probs(c, kt):
                for r in range(4):
                    last = tr(A[0:T, 2, T * r:T * (r + 1)], prob[:, r, T * kt:T * kt + T], ident_t)
                last.then_inc(pt_done[kt][c], 1)

            def weigh_values(c):
                b, g, half = combo(c)
                for r in range(4):
                    for kt in range(2):
                        w = WIDTH[kt]
                        last = mm(A[32 * r:32 * r + 32, 3, 0:T],
                                  v_sb[0:w, 2 * b + kt, 4 * g + r, :], probT[0:w, c % 2, kt, r, :],
                                  start=(kt == 0), stop=(kt == 1), tile_position=(0, 32 * r))
                last.then_inc(pv_done[c], 1)

            def attention(u, v, pixels):
                if u == 0:
                    pe.wait_ge(image_in, pixels)
                    pe.wait_ge(out_added, v)
                    conv(0, 4)
                if u == 1:
                    conv(4, HP).then_inc(conv_done, 1)
                if u == 3:
                    pe.wait_ge(raw_ready, v)
                    for j in range(4):
                        last = tr(A[0:T, 1, 128 * j:128 * j + 128], raw[:, START[j]:START[j] + T], perm_sb[:])
                    last.then_inc(raw_t, 1)
                if u == 6:
                    pe.wait_ge(xn1_ready, v)
                    tokens_to_features(A[:, 2, :], xn).then_inc(xn1_t, 1)
                if u in (7, 8):
                    if u == 7:
                        pe.wait_ge(xT1_ready, v)
                    for n in (2 * (u - 7), 2 * (u - 7) + 1):
                        mm(A[:, (3 + n) % 4, 0:PAIR], wqk_sb[:, n, :], xT1[:, 0:PAIR],
                           start=True, stop=True).then_inc(qk_done[n], 1)
                if u == 9:
                    pe.wait_ge(qk_ready[0], v)
                    for j in range(4):
                        last = mm(A[0:T, 3, 128 * j:128 * j + 128], xT1[:, START[j]:START[j] + T], wv_sb[:],
                                  start=True, stop=True)
                    last.then_inc(v_done, 1)
                if 11 <= u < 19:
                    c = u - 11
                    pe.wait_ge(exp_done[c], v)
                    if c:
                        pe.wait_ge(pt_ready[1][c - 1], v)
                    transpose_probs(c, 0)
                if 10 <= u < 18:
                    if u == 10:
                        for n in range(4):
                            pe.wait_ge(qk_ready[n], v)
                        pe.wait_ge(v_ready, v)
                    scores(u - 10)
                if 12 <= u < 20:
                    c = u - 12
                    pe.wait_ge(pt_ready[1][c], v)
                    if c:
                        pe.wait_ge(pv_read[c - 1], v)
                    weigh_values(c)
                if 11 <= u < 19:
                    c = u - 11
                    pe.wait_ge(pt_ready[0][c], v)
                    transpose_probs(c, 1)
                if u == 21:
                    pe.wait_ge(rwide_ready, v)
                    for g in range(2):
                        last = tokens_to_features(A[:, g, :], rwide[g])
                    last.then_inc(rwide_t, 1)
                if u == 22:
                    pe.wait_ge(heads_ready, v)
                    for j in range(4):
                        for g in range(2):
                            last = mm(A[0:T, 2, 128 * j:128 * j + 128], heads[:, g, START[j]:START[j] + T],
                                      wp_sb[:, g, :], start=(g == 0), stop=(g == 1))
                    last.then_inc(proj_done, 1)
                if u == 25:
                    pe.wait_ge(xn2_ready, v)
                    tokens_to_features(A[:, 0, :], xn).then_inc(xn2_t, 1)
                if u == 26:
                    pe.wait_ge(xT2_ready, v)
                    for j in range(4):
                        last = mm(A[0:T, 1, EXPERTS * j:EXPERTS * (j + 1)], xT2[:, START[j]:START[j] + T], wr_sb[:],
                                  start=True, stop=True)
                    last.then_inc(logits_done, 1)
                if u == 29:
                    pe.wait_ge(chosen_ready, v)
                    for j in range(5):
                        for i in range(min(j, 3) + 1):
                            kind = 0 if i == j else 1
                            last = mm(A[0:T, 2, EXPERTS * j:EXPERTS * (j + 1)], before_sb[0:WIDTH[i], kind, :],
                                      chosen[0:WIDTH[i], i, :], start=(i == 0), stop=(i == min(j, 3)))
                    last.then_inc(rank_done, 1)
                if u == 31:
                    pe.wait_ge(share_tok_ready, v)
                    tokens_to_features(A[:, 3, :], share_tok[:].bitcast(F32)).then_inc(share_t, 1)

            def expert_in(i, n1, v):
                if i == 0:
                    pe.wait_ge(x_lo_ready, v)
                pe.wait_ge(silu_done, n1)
                for w, xs, s, e in ((gate_hi, x_lo, True, False), (gate_lo, x_hi, False, False),
                                    (gate_hi, x_hi, False, True)):
                    last = mm(gate_ps[:, 0:PAIR], w[:, i, :], xs[:], start=s, stop=e)
                last.then_inc(gate_done, 1)
                pe.wait_ge(gated_done, n1)
                for w, xs, s, e in ((up_hi, x_lo, True, False), (up_lo, x_hi, False, False),
                                    (up_hi, x_hi, False, True)):
                    last = mm(up_ps[:, 0:PAIR], w[:, i, :], xs[:], start=s, stop=e)
                last.then_inc(up_done, 1)
                if i == 0:
                    pe.wait_ge(share_sb_ready, v)
                pe.wait_ge(hidden_done, n1)
                if i < ROUTED:
                    mm(share_ps[:, 0:PAIR], select_sb[:, i, :], share_sb[:], start=True, stop=True
                       ).then_inc(share_done, 1)
                else:
                    pe.nop().then_inc(share_done, 1)

            def expert_out(i):
                last = mm(y_ps[:, 0:PAIR], down_sb[:, i, :], hidden[:, i % 3, :],
                          start=(i == 0), stop=(i == UNITS - 1))
                if i == UNITS - 1:
                    last.then_inc(y_done, 1)

            def experts_and_attention(v, base, v_next, pixels):
                for i in range(UNITS):
                    expert_in(i, base + (i + 1), v)
                    if v_next is not None:
                        attention(i, v_next, pixels)
                    if i >= 2:
                        expert_out(i - 2)
                expert_out(UNITS - 2)
                pe.wait_ge(hidden_done, base + (UNITS + 1))
                expert_out(UNITS - 1)
                pe.wait_ge(y_read, v)
                for j in range(4):
                    last = tr(A[0:T, 0, 128 * j:128 * j + 128], y_sb[:, START[j]:START[j] + T], id_sb[:])
                last.then_inc(y_t, 1)

            pe.wait_ge(consts_in, 16 * 15)
            pe.wait_ge(presets, 5)
            for u in range(UNITS):
                attention(u, 1, IMAGE)
            pe.wait_ge(weights_in, 16)
            pe.wait_ge(split_step, 5)
            with pe.Fori(0, PAIRS - 1) as p:
                experts_and_attention(pe.snap(p + 1), pe.snap(p * UNITS), pe.snap(p + 2), IMAGE * (p + 2))
            experts_and_attention(PAIRS, (PAIRS - 1) * UNITS, None, None)

        @block.scalar
        def _(act):
            go = nc.scalar.activation

            def attention(u, v):
                if u == 1:
                    act.wait_ge(conv_done, v)
                    bank = A[:, 0, 0:2 * GRID * GRID]
                    for m, pad in ((0, pad_y), (1, pad_x)):
                        for to, of in ((64, 96), (96, 64)):
                            go(pad[to:to + 32, :, 1:1 + GRID, 1:1 + GRID],
                               bank[of:of + 32].rearrange("p (b t x) -> p b t x", b=2, x=GRID), ACT.Copy,
                               scale=mask_sb[of:of + 32, m:m + 1])
                    go(raw[:, 0:PAIR].rearrange("p (b n) -> p b n", b=2)[:, :, 1:NTOK],
                       bank.rearrange("p (b n) -> p b n", b=2), ACT.Identity, bias=conv_bias[:, 0:1]
                       ).then_inc(conv_read, 1)
                if u == 6:
                    act.wait_ge(xn1_t, v)
                    go(xT1[:, 0:PAIR], A[:, 2, 0:PAIR], ACT.Copy).then_inc(xT1_ready, 1)
                if u == 7:
                    act.wait_ge(qk_done[0], v)
                    go(q_sb[:, 0, 0:PAIR], A[:, 3, 0:PAIR], ACT.Copy, scale=HD ** -0.5).then_inc(qk_ready[0], 1)
                    act.wait_ge(qk_done[1], v)
                    for r in range(4):
                        last = go(k_sb[32 * r:32 * r + 32, 0, r, :], A[32 * r:32 * r + 32, 0, 0:PAIR], ACT.Copy)
                    last.then_inc(qk_ready[1], 1)
                if 10 <= u < 18:
                    c = u - 10
                    b, g, half = combo(c)
                    act.wait_ge(max_ready[c], v)
                    if c:
                        act.wait_ge(pt_done[1][c - 1], v)
                    for r in range(4):
                        last = go(prob[:, r, 0:NTOK], SCORES[:, r // 2, r % 2], ACT.Exp,
                                  bias=negmax[:, c, r:r + 1],
                                  accum_out=sums[:, 2 * b + half, 4 * g + r:4 * g + r + 1])
                    last.then_inc(exp_done[c], 1)
                if u == 25:
                    act.wait_ge(xn2_t, v)
                    go(xT2[:, 0:PAIR], A[:, 0, 0:PAIR], ACT.Copy).then_inc(xT2_ready, 1)
                if u == 27:
                    act.wait_ge(shifted_ready, v)
                    go(expl[:], shifted[:, :, 0:EXPERTS], ACT.Exp).then_inc(expl_ready, 1)

            def expert(i, n2):
                act.wait_ge(gate_done, n2)
                go(silu[:, i % 2, :], gate_ps[:, 0:PAIR], ACT.Silu).then_inc(silu_done, 1)

            def hand_over(v, units):
                act.wait_ge(up_done, units)
                act.wait_ge(xT2_ready, v)
                go(x_hi[:], xT2[:, 0:PAIR], ACT.Copy).then_inc(x_hi_ready, 1)
                act.wait_ge(share_t, v)
                go(share_sb[:], A[:, 3, 0:PAIR], ACT.Copy).then_inc(share_sb_ready, 1)

            def read_y(v):
                act.wait_ge(y_done, v)
                go(y_sb[:, 0:PAIR], y_ps[:, 0:PAIR], ACT.Copy).then_inc(y_read, 1)

            act.wait_ge(consts_in, 16 * 15)
            act.wait_ge(presets, 5)
            act.sem_inc(silu_done, 1)
            for u in range(UNITS):
                attention(u, 1)
            hand_over(1, 1)
            with act.Fori(0, PAIRS - 1) as p:
                base, v, v_next = act.snap(p * UNITS), act.snap(p + 1), act.snap(p + 2)
                for i in range(UNITS):
                    expert(i, base + (i + 2))
                    attention(i, v_next)
                hand_over(v_next, base + (UNITS + 1))
                read_y(v)
            for i in range(UNITS):
                expert(i, (PAIRS - 1) * UNITS + i + 2)
            read_y(PAIRS)

        @block.vector
        def _(dve):
            V = nc.vector

            def statistics(k, src, v):
                for j in range(4):
                    last = V.bn_stats(bn[:, k, j, :], src[:, j, :])
                last.then_inc(bn_done[k], 1)
                hold(dve, bn_done[k], v)
                for j in range(4):
                    last = V.bn_aggr(mv[:, k, j, :], bn[:, k, j, :])
                last.then_inc(var_ready[k], 1)

            def normalise(k, dst, src, v):
                dve.wait_ge(rstd_ready[k], v)
                for j in range(4):
                    last = V.tensor_scalar(dst[:, j, :], src[:, j, :], mv[:, k, j, 0:1], rstd[:, k, j:j + 1],
                                           ALU.subtract, ALU.mult)
                return last

            def attention(u, v, route):
                if u == 3:
                    dve.wait_ge(raw_t, v)
                    tok = A[0:T, 1, :].rearrange("p (j d) -> p j d", j=4)
                    statistics(0, tok, v)
                    normalise(0, xn, tok, v).then_inc(z_ready, 1)
                if u == 5:
                    dve.wait_ge(h0_ready, v)
                    statistics(1, h0, v)
                    normalise(1, xn, h0, v).then_inc(xn1_ready, 1)
                if u == 8:
                    dve.wait_ge(qk_done[2], v)
                    V.tensor_scalar(q_sb[:, 1, 0:PAIR], A[:, 1, 0:PAIR], HD ** -0.5, None, ALU.mult
                                    ).then_inc(qk_ready[2], 1)
                    dve.wait_ge(qk_done[3], v)
                    for r in range(4):
                        last = V.tensor_copy(k_sb[32 * r:32 * r + 32, 1, r, :], A[32 * r:32 * r + 32, 2, 0:PAIR])
                    last.then_inc(qk_ready[3], 1)
                if u == 9:
                    dve.wait_ge(v_done, v)
                    V.tensor_copy(v_sb[:, :, :, 0:HD], A[0:T, 3, :].rearrange("p (j h d) -> p j h d", j=4, h=HEADS)
                                  ).then_inc(v_ready, 1)
                if 11 <= u < 19:
                    c = u - 11
                    dve.wait_ge(pt_done[0][c], v)
                    V.tensor_copy(probT[:, c % 2, 0], A[0:T, 2, 0:4 * T].rearrange("p (r q) -> p r q", r=4)
                                  ).then_inc(pt_ready[0][c], 1)
                if 10 <= u < 18:
                    c = u - 10
                    dve.wait_ge(scores_done[c], v)
                    V.tensor_reduce(negmax[:, c, :].rearrange("p (a h) -> p a h", a=2), SCORES, AX_X, ALU.max,
                                    negate=True).then_inc(max_ready[c], 1)
                if 12 <= u < 20:
                    c = u - 12
                    b, g, half = combo(c)
                    j = 2 * b + half
                    dve.wait_ge(pv_done[c], v)
                    V.tensor_copy(heads[:, g, START[j]:START[j] + WIDTH[j]], A[:, 3, 0:WIDTH[j]]
                                  ).then_inc(pv_read[c], 1)
                if 11 <= u < 19:
                    c = u - 11
                    dve.wait_ge(pt_done[1][c], v)
                    V.tensor_copy(probT[:, c % 2, 1], A[0:T, 2, 0:4 * T].rearrange("p (r q) -> p r q", r=4)
                                  ).then_inc(pt_ready[1][c], 1)
                if u == 20:
                    dve.wait_ge(exp_done[7], v)
                    V.reciprocal(rinv[:], sums[:]).then_inc(rinv_done, 1)
                    dve.wait_ge(rinv_done, v)
                    dve.wait_ge(out_free, v)
                    for g in range(2):
                        for j in range(4):
                            last = V.tensor_copy(rwide[g][:, j, :].rearrange("p (r d) -> p r d", r=4),
                                                 rinv[:, j, 4 * g:4 * g + 4].unsqueeze(2).to_broadcast([T, 4, 32]))
                    last.then_inc(rwide_ready, 1)
                if u == 21:
                    dve.wait_ge(rwide_t, v)
                    dve.wait_ge(pv_read[7], v)
                    for g in range(2):
                        last = V.tensor_tensor(heads[:, g, 0:PAIR], heads[:, g, 0:PAIR], A[:, g, 0:PAIR], ALU.mult)
                    last.then_inc(heads_ready, 1)
                if u == 22:
                    dve.wait_ge(proj_done, v)
                    dve.wait_ge(h0_biased, v)
                    dve.wait_ge(resid_copied, v)
                    V.tensor_tensor(h1[:].rearrange("p j d -> p (j d)"), A[0:T, 2, :],
                                    h0[:].rearrange("p j d -> p (j d)"), ALU.add).then_inc(h1_ready, 1)
                if u == 23:
                    dve.wait_ge(h1_ready, v)
                    statistics(2, h1, v)
                    normalise(2, xn, h1, v).then_inc(xn2_ready, 1)
                if u == 26:
                    dve.wait_ge(logits_done, v)
                    V.tensor_tensor(logit[:], A[0:T, 1, 0:4 * EXPERTS].rearrange("p (j e) -> p j e", j=4),
                                    brout_sb[:].unsqueeze(1).to_broadcast([T, 4, EXPERTS]),
                                    ALU.add).then_inc(route_step, 1)
                    dve.wait_ge(route_step, route + 1)
                    V.tensor_reduce(lmax[:], logit[:], AX_X, ALU.max).then_inc(route_step, 1)
                    dve.wait_ge(route_step, route + 2)
                    V.tensor_tensor(logit[:], logit[:], lmax[:].unsqueeze(2).to_broadcast([T, 4, EXPERTS]),
                                    ALU.subtract).then_inc(route_step, 1)
                    dve.wait_ge(route_step, route + 3)
                    V.tensor_scalar(shifted[:, :, 0:EXPERTS], logit[:], LOWEST, None, ALU.max
                                    ).then_inc(shifted_ready, 1)
                if u == 27:
                    hold(dve, shifted_ready, v)
                    for j in range(4):
                        last = V.max(top8[:, j, :], shifted[:, j, 0:EXPERTS])
                    last.then_inc(route_step, 1)
                    dve.wait_ge(route_step, route + 4)
                    V.tensor_copy(topr[:, :, 0:TOPK], top8[:, :, 0:TOPK]).then_inc(route_step, 1)
                    hold(dve, route_step, route + 5)
                    for j in range(4):
                        last = V.match_replace(marked[:, j, :], topr[:, j, :], shifted[:, j, :], CHOSEN)
                    last.then_inc(route_step, 1)
                    dve.wait_ge(route_step, route + 6)
                    V.tensor_scalar(chosen[:], marked[:, :, 0:EXPERTS], CHOSEN, None, ALU.is_equal
                                    ).then_inc(chosen_ready, 1)
                if u == 28:
                    dve.wait_ge(expl_ready, v)
                    V.tensor_reduce(zsum[:, 0, :], expl[:], AX_X, ALU.add).then_inc(route_step, 1)
                    dve.wait_ge(route_step, route + 7)
                    V.scalar_tensor_tensor(expc[:], marked[:, :, 0:EXPERTS], CHOSEN, expl[:], ALU.is_equal, ALU.mult
                                           ).then_inc(expc_ready, 1)
                    dve.wait_ge(expc_ready, v)
                    V.tensor_reduce(zsum[:, 1, :], expc[:], AX_X, ALU.add).then_inc(zsum_ready, 1)
                    dve.wait_ge(zsum_ready, v)
                    V.scalar_tensor_tensor(zsum[:, 2, :], zsum[:, 0, :], GATE_EPS, zsum[:, 1, :], ALU.mult, ALU.add
                                           ).then_inc(den_ready, 1)
                    dve.wait_ge(den_ready, v)
                    V.reciprocal(rden[:], zsum[:, 2, :]).then_inc(rden_ready, 1)
                if u == 29:
                    dve.wait_ge(rank_done, v)
                    V.tensor_tensor(slot[:], A[0:T, 2, 0:4 * EXPERTS].rearrange("p (j e) -> p j e", j=4),
                                    counts[:].unsqueeze(1).to_broadcast([T, 4, EXPERTS]), ALU.add
                                    ).then_inc(slot_ready, 1)
                    dve.wait_ge(slot_ready, v)
                    V.tensor_tensor(counts[:], A[0:T, 2, 4 * EXPERTS:5 * EXPERTS], counts[:], ALU.add)
                    V.scalar_tensor_tensor(kept, slot[:], CAPACITY, expc[:], ALU.is_lt, ALU.mult
                                           ).then_inc(kept_ready, 1)
                    dve.wait_ge(kept_ready, v)
                    dve.wait_ge(rden_ready, v)
                    V.tensor_tensor(slot[:], kept, rden[:].unsqueeze(2).to_broadcast([T, 4, EXPERTS]), ALU.mult
                                    ).then_inc(share_ready, 1)
                if u == 30:
                    dve.wait_ge(share_ready, v)
                    V.tensor_copy(share_tok[:, :, 0:EXPERTS], slot[:]).then_inc(share_hi, 1)
                    dve.wait_ge(share_hi, v)
                    V.tensor_tensor(share_tok[:, :, EXPERTS:], slot[:], share_tok[:, :, 0:EXPERTS].bitcast(F32),
                                    ALU.subtract).then_inc(share_tok_ready, 1)

            def expert(i, n2):
                dve.wait_ge(up_done, n2)
                dve.wait_ge(silu_done, n2)
                V.tensor_tensor(hidden[:, i % 3, :], silu[:, i % 2, :], up_ps[:, 0:PAIR], ALU.mult
                                ).then_inc(gated_done, 1)
                dve.wait_ge(gated_done, n2)
                if i < ROUTED:
                    dve.wait_ge(share_done, n2)
                    V.tensor_tensor(hidden[:, i % 3, :], hidden[:, i % 3, :], share_ps[:, 0:PAIR], ALU.mult
                                    ).then_inc(hidden_done, 1)
                else:
                    V.tensor_scalar(hidden[:, i % 3, :], hidden[:, i % 3, :], 0.5, None, ALU.mult
                                    ).then_inc(hidden_done, 1)

            def add_output(v):
                dve.wait_ge(y_t, v)
                dve.wait_ge(resid_copied, v + 1)
                dve.wait_ge(out_free, v + 1)
                V.tensor_tensor(out_sb[:].rearrange("p j d -> p (j d)"), A[0:T, 0, :],
                                resid[:].rearrange("p j d -> p (j d)"), ALU.add).then_inc(out_added, 1)

            for t in (raw[:], pad_y[:], pad_x[:], xT1[:], q_sb[:], k_sb[:], v_sb[:], prob[:], heads[:], xT2[:], counts[:]):
                V.memset(t, 0.0)
            V.memset(topr[:], FILLER)
            V.memset(shifted[:], FILLER)
            V.memset(half_neg[:], -0.5).then_inc(presets, 4)
            dve.sem_inc(gated_done, 1)
            dve.sem_inc(hidden_done, 1)
            dve.sem_inc(gate_done, 1)
            dve.sem_inc(up_done, 1)
            dve.sem_inc(share_done, 1)
            dve.sem_inc(out_added, CREDITS_Y)
            dve.sem_inc(out_free, CREDITS_Y)
            dve.sem_inc(resid_copied, 1)
            dve.wait_ge(consts_in, 16 * 15)
            V.tensor_copy(before_sb[:], before_f).then_inc(presets, 1)
            dve.wait_ge(presets, 5)
            for n, (hi, lo) in enumerate(((gate_hi, gate_lo), (up_hi, up_lo))):
                flat = hi[:].rearrange("p u m -> p (u m)")
                dve.wait_ge(stage_in, 16 * (n + 1))
                V.tensor_copy(flat, stage).then_inc(split_step, 1)
                dve.wait_ge(split_step, 2 * n + 1)
                V.tensor_tensor(lo[:].rearrange("p u m -> p (u m)"), stage, flat.bitcast(F32), ALU.subtract
                                ).then_inc(split_step, 1)
            dve.wait_ge(stage_in, 48)
            V.tensor_copy(select_sb[:].rearrange("p u m -> p (u m)"), stage[:, 0:ROUTED * 128]).then_inc(split_step, 1)

            for u in range(UNITS):
                attention(u, 1, 0)
            with dve.Fori(0, PAIRS - 1) as p:
                base, v, v_next = dve.snap(p * UNITS), dve.snap(p + 1), dve.snap(p + 2)
                route = dve.snap(ROUTE_STEPS * (p + 1))
                for i in range(UNITS):
                    expert(i, base + (i + 2))
                    attention(i, v_next, route)
                add_output(v)
            for i in range(UNITS):
                expert(i, (PAIRS - 1) * UNITS + i + 2)
            add_output(PAIRS)

        @block.gpsimd
        def _(pool):
            G = nc.gpsimd

            def root(k, v):
                hold(pool, var_ready[k], v)
                G.tensor_scalar(var_eps[:, k, :], mv[:, k, :, 1], EPS, None, ALU.add).then_inc(eps_added[k], 1)
                pool.wait_ge(eps_added[k], v)
                G.tensor_tensor(rstd[:, k, :], var_eps[:, k, :], half_neg[:], ALU.pow).then_inc(rstd_ready[k], 1)

            def attention(u, v):
                if u == 1:
                    pool.wait_ge(resid_copied, v)
                    pool.wait_ge(conv_read, v)
                    for pad, sem_, places in ((pad_y, raw_step, ((64, 2, 1), (96, 0, 1))),
                                              (pad_x, raw_ready, ((64, 1, 2), (96, 1, 0)))):
                        for at, dy, dx in places:
                            dst = raw[at:at + 32, 0:PAIR].rearrange("p (b n) -> p b n", b=2)[:, :, 1:NTOK].rearrange(
                                "p b (t x) -> p b t x", x=GRID)
                            last = G.tensor_tensor(dst, dst, pad[at:at + 32, :, dy:dy + GRID, dx:dx + GRID], ALU.add)
                        last.then_inc(sem_, 1)
                        if sem_ is raw_step:
                            pool.wait_ge(raw_step, v)
                if u == 3:
                    root(0, v)
                    pool.wait_ge(z_ready, v)
                    G.tensor_tensor(xn[:], xn[:], lng_sb[:].unsqueeze(1).to_broadcast([T, 4, 128]), ALU.mult
                                    ).then_inc(scaled, 1)
                    pool.wait_ge(scaled, v)
                    G.tensor_tensor(h0[:], xn[:], lnb_sb[:].unsqueeze(1).to_broadcast([T, 4, 128]), ALU.add).then_inc(shifted_h0, 1)
                    hold(pool, shifted_h0, v)
                    G.tensor_copy(h0[0:1, 2, :], cls_sb[:])
                    G.tensor_copy(h0[0:1, 0, :], cls_sb[:]).then_inc(h0_ready, 1)
                if u == 5:
                    root(1, v)
                    pool.wait_ge(xn1_ready, v)
                    G.tensor_tensor(h0[:], h0[:], bproj_sb[:].unsqueeze(1).to_broadcast([T, 4, 128]), ALU.add).then_inc(h0_biased, 1)
                if u == 23:
                    root(2, v)

            def hand_over(v):
                pool.wait_ge(x_hi_ready, v)
                G.tensor_tensor(x_lo[:], xT2[:, 0:PAIR], x_hi[:].bitcast(F32), ALU.subtract).then_inc(x_lo_ready, 1)
                pool.wait_ge(h1_ready, v)
                hold(pool, out_added, v + 1)
                G.tensor_copy(resid[:], h1[:]).then_inc(resid_copied, 1)

            pool.wait_ge(consts_in, 16 * 15)
            pool.wait_ge(presets, 5)
            for u in range(UNITS):
                attention(u, 1)
            hand_over(1)
            with pool.Fori(0, PAIRS - 1) as p:
                v_next = pool.snap(p + 2)
                for i in range(UNITS):
                    attention(i, v_next)
                hand_over(v_next)


def kernel(**inputs):
    import numpy as np
    import concourse.bacc as bacc
    from concourse.bass_utils import run_bass_kernel_spmd as run

    a = {k: np.asarray(v) for k, v in inputs.items()}
    f4 = np.float32
    P = PS

    main = a["L0_tok_W_main"].reshape(64, 3, P, 2, HP).transpose(3, 1, 2, 4, 0)
    sy = a["L0_tok_W_sy"].reshape(16, 3, P, 2, HP).transpose(3, 1, 2, 4, 0)
    sx = a["L0_tok_W_sx"].reshape(16, 3, P, 2, HP).transpose(3, 1, 2, 4, 0)
    conv = np.zeros((2, 3, P, HP, 128), f4)
    conv[..., 0:64] = main
    conv[:, :, HP:, :, 64:80] = sy[:, :, :HP]
    conv[1, ..., 80:96] = sx[0]
    conv[:, :, :HP, :, 96:112] = sy[:, :, HP:]
    conv[0, ..., 112:128] = sx[1]
    bm, bx, by = a["L0_tok_b_main"], a["L0_tok_b_sx"], a["L0_tok_b_sy"]
    conv_b = np.concatenate([bm, by, bx, by, bx]).reshape(128, 1)
    masks = np.zeros((4, 2, 16, 2), f4)
    masks[:, 0, :, 0] = 1
    masks[:, 1, :, 1] = 1
    perm = np.zeros((128, 128), f4)
    order = np.concatenate([np.arange(64), np.arange(96, 112), np.arange(64, 80), np.arange(112, 128),
                            np.arange(80, 96)])
    perm[np.arange(128), order] = 1

    qkv = a["L0_attn_w_qkv"].reshape(3, 2, 4, HD, D)
    w_qk = np.zeros((D, 2, 2, 4, 32), f4)
    w_qk[..., 0:HD] = qkv[0:2].transpose(4, 1, 0, 2, 3)
    w_p = np.zeros((2, 4, 32, D), f4)
    w_p[:, :, 0:HD, :] = a["L0_attn_w_proj"].T.reshape(2, 4, HD, D)

    def by_feature(routed, shared):
        return np.concatenate([routed.reshape(-1, D), shared.reshape(-1, D)]).T

    down = np.concatenate([a["L0_ffn_w_down"], a["L0_ffn_shared_w_down"]]).transpose(0, 2, 1)
    select = np.zeros((2, EXPERTS, EXPERTS, F), f4)
    select[:, np.arange(EXPERTS), np.arange(EXPERTS), :] = 1
    before = np.ones((T, 2, T), f4)
    before[:, 0, :] = np.triu(np.ones((T, T), f4), 1)

    arrays = {
        "x": a["x"], "conv_w": conv.reshape(96, HP * 128), "conv_b": conv_b, "masks": masks.reshape(128, 2),
        "perm": perm, "ident": np.eye(128, dtype=f4), "cls_tok": a["cls_tok"].reshape(1, D),
        "ln_g": np.broadcast_to(a["L0_tok_ln_g"], (T, D)), "ln_b": np.broadcast_to(a["L0_tok_ln_b"], (T, D)),
        "w_qk": w_qk.reshape(D, 512), "w_v": qkv[2].reshape(D, D).T,
        "w_p": w_p.reshape(2, 128, D).transpose(1, 0, 2).reshape(128, 256),
        "b_proj": np.broadcast_to(a["L0_attn_b_proj"], (T, D)),
        "w_r": a["L0_ffn_router_w"].T, "b_r": np.broadcast_to(a["L0_ffn_bias"], (T, EXPERTS)),
        "w_gate": by_feature(a["L0_ffn_w_gate"], a["L0_ffn_shared_w_gate"]),
        "w_up": by_feature(a["L0_ffn_w_up"], a["L0_ffn_shared_w_up"]),
        "w_down": down.reshape(UNITS, 128, D).transpose(1, 0, 2).reshape(128, UNITS * D),
        "select": select.reshape(128, EXPERTS * F), "before": before.reshape(T, 2 * T),
    }
    arrays = {k: np.ascontiguousarray(v) for k, v in arrays.items()}
    nc = bacc.Bacc("TRN2", target_bir_lowering=False, num_devices=1)
    args = [nc.dram_tensor(f"in_{k}", v.shape, mybir.dt.from_np(v.dtype), kind="ExternalInput").ap()
            for k, v in arrays.items()]
    shape = (a["x"].shape[0], NTOK, D)
    args.append(nc.dram_tensor("out_0", shape, F32, kind="ExternalOutput").ap())
    vit_layer(nc, **dict(zip(list(arrays) + ["out"], args)))
    r = run(nc, [{f"in_{k}": v for k, v in arrays.items()}], core_ids=[0])
    return r.results[0]["out_0"]
```

```python
from contextlib import ExitStack

import concourse.bass as bass
from concourse import mybir

F32 = mybir.dt.float32
F32R = mybir.dt.float32r
BF16 = mybir.dt.bfloat16
ALU = mybir.AluOpType
ACT = mybir.ActivationFunctionType
AX_X = mybir.AxisListType.X

D = 128
HEADS, HD = 8, 16
PS, HP = 16, 8
GRID = 14
NTOK = 1 + GRID * GRID
PAIR = 2 * NTOK
COLS = PAIR + 2
T = 99
START = [0, T, NTOK, NTOK + T]
WIDTH = [T, NTOK - T, T, NTOK - T]
EXPERTS, TOPK, F = 64, 6, 64
ROUTED = EXPERTS // 2
UNITS = ROUTED + 1
EPS = 1e-5
GATE_EPS = 1e-9
LOWEST = -104.0
FILLER = -1e30
CHOSEN = 1.0
CREDITS_Y = 2
ROUTE_STEPS = 13
CONV_AT = {22: 1, 23: 2, 25: 1, 26: 2, 27: 1, 28: 1}


def vit_layer(nc, x, conv_w, conv_b, masks, perm, ident, cls_tok, ln_g, ln_b, w_qk, w_v, w_p, b_proj,
              w_r, b_r, w_gate, w_up, w_down, select, before, out):
    B = x.shape[0]
    PAIRS = B // 2
    CAPACITY = float(max(1, int(B * NTOK * TOPK * 2.0 / EXPERTS)))

    with ExitStack() as ctx:
        def sb(name, shape, dt=F32):
            return ctx.enter_context(nc.sbuf_tensor(name, shape, dt))

        def sem(name):
            return ctx.enter_context(nc.semaphore(name))

        def sems(name, n):
            return [sem(f"{name}{i}") for i in range(n)]

        gate_ps = ctx.enter_context(nc.psum_tensor("gate_ps", [128, 512], F32))
        up_ps = ctx.enter_context(nc.psum_tensor("up_ps", [128, 512], F32))
        share_ps = ctx.enter_context(nc.psum_tensor("share_ps", [128, 512], F32))
        y_ps = ctx.enter_context(nc.psum_tensor("y_ps", [128, 512], F32))
        A = ctx.enter_context(nc.psum_tensor("A", [128, 4, 512], F32))
        SCORES = A[0:T, 0:2, 0:PAIR].rearrange("p a (h k) -> p a h k", h=2)

        conv_sb = sb("conv_sb", [96, HP, 128])
        conv_bias = sb("conv_bias", [128, 1])
        mask_sb = sb("mask_sb", [128, 2])
        perm_sb = sb("perm_sb", [128, 128])
        id_sb = sb("id_sb", [128, 128])
        cls_sb = sb("cls_sb", [1, 128])
        lng_sb = sb("lng_sb", [T, 128])
        lnb_sb = sb("lnb_sb", [T, 128])
        bproj_sb = sb("bproj_sb", [T, 128])
        brout_sb = sb("brout_sb", [T, EXPERTS])
        wqk_sb = sb("wqk_sb", [128, 4, 128])
        wv_sb = sb("wv_sb", [128, 128])
        wp_sb = sb("wp_sb", [128, 2, 128])
        wr_sb = sb("wr_sb", [128, EXPERTS])
        before_sb = sb("before_sb", [T, 2, T], BF16)
        half_neg = sb("half_neg", [T, 4])
        gate_hi = sb("gate_hi", [128, UNITS, 128], F32R)
        gate_lo = sb("gate_lo", [128, UNITS, 128], F32R)
        up_hi = sb("up_hi", [128, UNITS, 128], F32R)
        up_lo = sb("up_lo", [128, UNITS, 128], F32R)
        down_sb = sb("down_sb", [128, UNITS, 128])
        stage = down_sb[:].rearrange("p u m -> p (u m)")
        select_sb = sb("select_sb", [128, ROUTED, 128], F32R)

        image = sb("image", [96, 2 * GRID, GRID * PS])
        raw = sb("raw", [128, COLS])
        pad_y = sb("pad_y", [128, 2, 16, 16])
        pad_x = sb("pad_x", [128, 2, 16, 16])
        bn = sb("bn", [T, 3, 4, 6])
        mv = sb("mv", [T, 3, 4, 2])
        var_eps = sb("var_eps", [T, 3, 4])
        rstd = sb("rstd", [T, 3, 4])
        h0 = sb("h0", [T, 4, 128])
        xn = sb("xn", [T, 4, 128])
        xT1 = sb("xT1", [128, COLS])
        q_sb = sb("q_sb", [128, 2, COLS])
        k_sb = sb("k_sb", [128, 2, 4, PAIR])
        v_sb = sb("v_sb", [T, 4, HEADS, 32])
        negmax = sb("negmax", [T, 8, 4])
        sums = sb("sums", [T, 4, HEADS])
        rinv = sb("rinv", [T, 4, HEADS])
        out_sb = sb("out_sb", [T, 4, 128])
        rwide = [xn, out_sb]
        prob = sb("prob", [T, 4, NTOK + 1])
        probT = sb("probT", [T, 2, 2, 4, T])
        heads = sb("heads", [128, 2, COLS])
        h1 = sb("h1", [T, 4, 128])
        before_f = h1[:].rearrange("p j d -> p (j d)")[:, 0:2 * T].rearrange("p (a b) -> p a b", a=2)
        resid = sb("resid", [T, 4, 128])
        xT2 = sb("xT2", [128, COLS])
        logit = sb("logit", [T, 4, EXPERTS])
        lmax = sb("lmax", [T, 4])
        shifted = sb("shifted", [T, 4, EXPERTS + 2])
        marked = sb("marked", [T, 4, EXPERTS + 2])
        top8 = sb("top8", [T, 4, 8])
        topr = sb("topr", [T, 4, 8])
        chosen = sb("chosen", [T, 4, EXPERTS], BF16)
        expl = sb("expl", [T, 4, EXPERTS])
        expc = expl
        zsum = sb("zsum", [T, 3, 4])
        rden = sb("rden", [T, 4])
        slot = logit
        kept = marked[:, :, 0:EXPERTS]
        counts = sb("counts", [T, EXPERTS])
        share_tok = sb("share_tok", [T, 4, 128], F32R)
        share_sb = sb("share_sb", [128, PAIR], F32R)
        x_hi = sb("x_hi", [128, PAIR], F32R)
        x_lo = sb("x_lo", [128, PAIR], F32R)
        tanh = sb("tanh", [128, 2, PAIR])
        hidden = sb("hidden", [128, 3, PAIR])
        y_sb = heads[:, 0, :]

        consts_in = sem("consts_in")
        weights_in = sem("weights_in")
        stage_in = sem("stage_in")
        split_step = sem("split_step")
        presets = sem("presets")
        image_in = sem("image_in")
        conv_done = sem("conv_done")
        conv_read = sem("conv_read")
        raw_step = sem("raw_step")
        raw_ready = sem("raw_ready")
        raw_t = sem("raw_t")
        bn_done = sems("bn_done", 3)
        var_ready = sems("var_ready", 3)
        eps_added = sems("eps_added", 3)
        rstd_ready = sems("rstd_ready", 3)
        z_ready = sem("z_ready")
        scaled = sem("scaled")
        shifted_h0 = sem("shifted_h0")
        h0_ready = sem("h0_ready")
        h0_biased = sem("h0_biased")
        xn1_ready = sem("xn1_ready")
        xn1_t = sem("xn1_t")
        xT1_ready = sem("xT1_ready")
        qk_done = sems("qk_done", 4)
        qk_ready = sems("qk_ready", 4)
        v_done = sem("v_done")
        v_ready = sem("v_ready")
        scores_done = sems("scores_done", 8)
        max_ready = sems("max_ready", 8)
        exp_done = sems("exp_done", 8)
        pt_done = [sems("pt_done_a", 8), sems("pt_done_b", 8)]
        pt_ready = [sems("pt_ready_a", 8), sems("pt_ready_b", 8)]
        pv_done = sems("pv_done", 8)
        pv_read = sems("pv_read", 8)
        rinv_done = sem("rinv_done")
        rwide_ready = sem("rwide_ready")
        rwide_t = sem("rwide_t")
        heads_ready = sem("heads_ready")
        proj_done = sem("proj_done")
        h1_ready = sem("h1_ready")
        xn2_ready = sem("xn2_ready")
        xn2_t = sem("xn2_t")
        xT2_ready = sem("xT2_ready")
        logits_done = sem("logits_done")
        route_step = sem("route_step")
        shifted_ready = sem("shifted_ready")
        chosen_ready = sem("chosen_ready")
        expl_ready = sem("expl_ready")
        rden_ready = sem("rden_ready")
        rank_done = sem("rank_done")
        share_hi = sem("share_hi")
        share_tok_ready = sem("share_tok_ready")
        share_t = sem("share_t")
        share_sb_ready = sem("share_sb_ready")
        x_hi_ready = sem("x_hi_ready")
        x_lo_ready = sem("x_lo_ready")
        resid_copied = sem("resid_copied")
        gate_done = sem("gate_done")
        up_done = sem("up_done")
        share_done = sem("share_done")
        tanh_done = sem("tanh_done")
        silu_done = sem("silu_done")
        gated_done = sem("gated_done")
        hidden_done = sem("hidden_done")
        y_done = sem("y_done")
        y_read = sem("y_read")
        y_t = sem("y_t")
        out_added = sem("out_added")
        out_stored = sem("out_stored")
        out_free = sem("out_free")

        NCONST = 17
        x_view = x.rearrange("(p b) c (t y) x -> p c y b t x", b=2, y=PS)
        out_view = out.rearrange("(p b) t d -> p t b d", b=2)
        IMAGE = 12 * 16
        STORED = 2 * 16

        def combo(c):
            return c // 4, c // 2 % 2, c % 2

        def hold(eng, sem_, value):
            eng.wait_ge(sem_, value)
            eng.nop(nofuse=True)

        block = ctx.enter_context(nc.Block())

        @block.sync
        def _(sp):
            for dst, src in ((conv_sb[:], conv_w.rearrange("p (a b) -> p a b", a=HP)),
                             (conv_bias[:], conv_b), (mask_sb[:], masks), (perm_sb[:], perm),
                             (id_sb[:], ident), (cls_sb[:], cls_tok),
                             (wqk_sb[:], w_qk.rearrange("p (a b) -> p a b", a=4)), (wv_sb[:], w_v),
                             (wp_sb[:], w_p.rearrange("p (a b) -> p a b", a=2)), (wr_sb[:], w_r),
                             (before_f, before.rearrange("p (a b) -> p a b", a=2))):
                sp.dma_start(dst, src).then_inc(consts_in, 16)

            def load_image(p):
                for g in range(2):
                    w = GRID * PS - HP * g
                    for c in range(3):
                        for b in range(2):
                            sp.dma_start(image[48 * g + 16 * c:48 * g + 16 * c + 16, GRID * b:GRID * (b + 1), 0:w],
                                         x_view[p, c, :, b, :, HP * g:HP * g + w]).then_inc(image_in, 16)

            load_image(0)
            for dst, src in ((lng_sb, ln_g), (lnb_sb, ln_b), (bproj_sb, b_proj), (brout_sb, b_r)):
                sp.dma_start(dst[:], src).then_inc(consts_in, 16)
            sp.dma_start(stage, w_gate).then_inc(stage_in, 16)
            sp.wait_ge(split_step, 2)
            sp.dma_start(stage, w_up).then_inc(stage_in, 16)
            sp.wait_ge(split_step, 4)
            sp.dma_start(stage[:, 0:ROUTED * 128], select).then_inc(stage_in, 16)
            sp.wait_ge(split_step, 5)
            sp.dma_start(stage, w_down).then_inc(weights_in, 16)
            sp.wait_ge(conv_done, 1)
            load_image(1)

            def store(p):
                sp.wait_ge(out_added, p + 1 + CREDITS_Y)
                for half in range(2):
                    w = WIDTH[half]
                    sp.dma_start(out_view[p, T * half:T * half + w],
                                 out_sb[0:w].rearrange("t (b h) d -> t h b d", h=2)[:, half]
                                 ).then_inc(out_stored, 16)
                sp.wait_ge(out_stored, STORED * (p + 1))
                sp.sem_inc(out_free, 1)

            with sp.Fori(0, PAIRS - 2) as p:
                sp.wait_ge(conv_done, p + 2)
                load_image(p + 2)
                store(p)
            store(PAIRS - 2)
            store(PAIRS - 1)

        @block.tensor
        def _(pe):
            mm, tr = nc.tensor.matmul, nc.tensor.transpose
            ident_t = id_sb[0:T, 0:T]

            def conv(lo, hi):
                for px in range(lo, hi):
                    last = mm(A[:, 0, 0:2 * GRID * GRID].rearrange("p (t x) -> p t x", x=GRID),
                              conv_sb[:, px, :],
                              image[:].rearrange("p t (x q) -> p t x q", q=PS)[:, :, :, px],
                              start=(px == 0), stop=(px == HP - 1))
                return last

            def tokens_to_features(dst, src):
                for j in range(4):
                    w = WIDTH[j]
                    last = tr(dst[:, START[j]:START[j] + w], src[0:w, j, :], id_sb[0:w, 0:w])
                return last

            def scores(c):
                b, g, half = combo(c)
                j = 2 * b + half
                for r in range(4):
                    last = mm(SCORES[:, r // 2, r % 2], q_sb[:, g, START[j]:START[j] + T],
                              k_sb[:, g, r, NTOK * b:NTOK * (b + 1)], start=True, stop=True)
                last.then_inc(scores_done[c], 1)

            def transpose_probs(c, kt):
                for r in range(4):
                    last = tr(A[0:T, 2, T * r:T * (r + 1)], prob[:, r, T * kt:T * kt + T], ident_t)
                last.then_inc(pt_done[kt][c], 1)

            def weigh_values(c):
                b, g, half = combo(c)
                for r in range(4):
                    for kt in range(2):
                        w = WIDTH[kt]
                        last = mm(A[32 * r:32 * r + 32, 3, 0:T],
                                  v_sb[0:w, 2 * b + kt, 4 * g + r, :], probT[0:w, c % 2, kt, r, :],
                                  start=(kt == 0), stop=(kt == 1), tile_position=(0, 32 * r))
                last.then_inc(pv_done[c], 1)

            def conv_part(u, pixels):
                if u in CONV_AT:
                    lo = sum(n for at, n in CONV_AT.items() if at < u)
                    if lo == 0:
                        pe.wait_ge(image_in, pixels)
                    last = conv(lo, lo + CONV_AT[u])
                    if lo + CONV_AT[u] == HP:
                        last.then_inc(conv_done, 1)

            def attention(u, v):
                if u == 1:
                    pe.wait_ge(raw_ready, v)
                    for j in range(4):
                        last = tr(A[0:T, 1, 128 * j:128 * j + 128], raw[:, START[j]:START[j] + T], perm_sb[:])
                    last.then_inc(raw_t, 1)
                if u == 6:
                    pe.wait_ge(xn1_ready, v)
                    pe.wait_ge(out_added, v)
                    tokens_to_features(A[:, 2, :], xn).then_inc(xn1_t, 1)
                if u in (7, 8):
                    if u == 7:
                        pe.wait_ge(xT1_ready, v)
                    for n in (2 * (u - 7), 2 * (u - 7) + 1):
                        mm(A[:, (3 + n) % 4, 0:PAIR], wqk_sb[:, n, :], xT1[:, 0:PAIR],
                           start=True, stop=True).then_inc(qk_done[n], 1)
                if u == 9:
                    pe.wait_ge(qk_ready[0], v)
                    for j in range(4):
                        last = mm(A[0:T, 3, 128 * j:128 * j + 128], xT1[:, START[j]:START[j] + T], wv_sb[:],
                                  start=True, stop=True)
                    last.then_inc(v_done, 1)
                if 11 <= u < 19:
                    c = u - 11
                    pe.wait_ge(exp_done[c], v)
                    if c:
                        pe.wait_ge(pt_ready[1][c - 1], v)
                    transpose_probs(c, 0)
                if 10 <= u < 18:
                    if u == 10:
                        for n in range(4):
                            pe.wait_ge(qk_ready[n], v)
                        pe.wait_ge(v_ready, v)
                    scores(u - 10)
                if 11 <= u < 19:
                    c = u - 11
                    pe.wait_ge(pt_ready[0][c], v)
                    transpose_probs(c, 1)
                if 12 <= u < 20:
                    c = u - 12
                    if c == 7:
                        pe.wait_ge(pt_ready[1][c], v)
                    if c:
                        pe.wait_ge(pv_read[c - 1], v)
                    weigh_values(c)
                if u == 20:
                    pe.wait_ge(rwide_ready, v)
                    for g in range(2):
                        last = tokens_to_features(A[:, g, :], rwide[g])
                    last.then_inc(rwide_t, 1)
                if u == 21:
                    pe.wait_ge(heads_ready, v)
                    for j in range(4):
                        for g in range(2):
                            last = mm(A[0:T, 2, 128 * j:128 * j + 128], heads[:, g, START[j]:START[j] + T],
                                      wp_sb[:, g, :], start=(g == 0), stop=(g == 1))
                    last.then_inc(proj_done, 1)
                if u == 24:
                    pe.wait_ge(xn2_ready, v)
                    tokens_to_features(A[:, 1, :], xn).then_inc(xn2_t, 1)
                if u == 25:
                    pe.wait_ge(xT2_ready, v)
                    for j in range(4):
                        last = mm(A[0:T, 3, EXPERTS * j:EXPERTS * (j + 1)], xT2[:, START[j]:START[j] + T], wr_sb[:],
                                  start=True, stop=True)
                    last.then_inc(logits_done, 1)
                if u == 28:
                    pe.wait_ge(chosen_ready, v)
                    for j in range(5):
                        for i in range(min(j, 3) + 1):
                            kind = 0 if i == j else 1
                            last = mm(A[0:T, 2, EXPERTS * j:EXPERTS * (j + 1)], before_sb[0:WIDTH[i], kind, :],
                                      chosen[0:WIDTH[i], i, :], start=(i == 0), stop=(i == min(j, 3)))
                    last.then_inc(rank_done, 1)
                if u == 31:
                    pe.wait_ge(share_tok_ready, v)
                    tokens_to_features(A[:, 3, :], share_tok[:].bitcast(F32)).then_inc(share_t, 1)

            def expert_in(i, n1, v):
                if i == 0:
                    pe.wait_ge(x_lo_ready, v)
                pe.wait_ge(silu_done, n1)
                for w, xs, s, e in ((gate_hi, x_lo, True, False), (gate_lo, x_hi, False, False),
                                    (gate_hi, x_hi, False, True)):
                    last = mm(gate_ps[:, 0:PAIR], w[:, i, :], xs[:], start=s, stop=e)
                last.then_inc(gate_done, 1)
                pe.wait_ge(gated_done, n1)
                for w, xs, s, e in ((up_hi, x_lo, True, False), (up_lo, x_hi, False, False),
                                    (up_hi, x_hi, False, True)):
                    last = mm(up_ps[:, 0:PAIR], w[:, i, :], xs[:], start=s, stop=e)
                last.then_inc(up_done, 1)
                if i == 0:
                    pe.wait_ge(share_sb_ready, v)
                pe.wait_ge(hidden_done, n1)
                if i < ROUTED:
                    mm(share_ps[:, 0:PAIR], select_sb[:, i, :], share_sb[:], start=True, stop=True
                       ).then_inc(share_done, 1)
                else:
                    pe.nop().then_inc(share_done, 1)

            def expert_out(i):
                last = mm(y_ps[:, 0:PAIR], down_sb[:, i, :], hidden[:, i % 3, :],
                          start=(i == 0), stop=(i == UNITS - 1))
                if i == UNITS - 1:
                    last.then_inc(y_done, 1)

            def experts_and_attention(v, base, v_next, pixels):
                for i in range(UNITS):
                    expert_in(i, base + (i + 1), v)
                    if v_next is not None:
                        attention(i, v_next)
                    if pixels is not None:
                        conv_part(i, pixels)
                    if i >= 2:
                        expert_out(i - 2)
                expert_out(UNITS - 2)
                pe.wait_ge(hidden_done, base + (UNITS + 1))
                expert_out(UNITS - 1)
                pe.wait_ge(y_read, v)
                for j in range(4):
                    last = tr(A[0:T, 2, 128 * j:128 * j + 128], y_sb[:, START[j]:START[j] + T], id_sb[:])
                last.then_inc(y_t, 1)

            pe.wait_ge(consts_in, 16 * 15)
            pe.wait_ge(presets, 5)
            pe.wait_ge(image_in, IMAGE)
            conv(0, HP).then_inc(conv_done, 1)
            for u in range(UNITS):
                attention(u, 1)
                conv_part(u, 2 * IMAGE)
            pe.wait_ge(weights_in, 16)
            pe.wait_ge(split_step, 5)
            with pe.Fori(0, PAIRS - 2) as p:
                experts_and_attention(pe.snap(p + 1), pe.snap(p * UNITS), pe.snap(p + 2), IMAGE * (p + 3))
            experts_and_attention(PAIRS - 1, (PAIRS - 2) * UNITS, PAIRS, None)
            experts_and_attention(PAIRS, (PAIRS - 1) * UNITS, None, None)

        @block.scalar
        def _(act):
            go = nc.scalar.activation

            def patches(part, v):
                bank = A[:, 0, 0:2 * GRID * GRID]
                if part == 0:
                    act.wait_ge(conv_done, v)
                if part < 2:
                    pad = (pad_y, pad_x)[part]
                    for to, of in ((64, 96), (96, 64)):
                        go(pad[to:to + 32, :, 1:1 + GRID, 1:1 + GRID],
                           bank[of:of + 32].rearrange("p (b t x) -> p b t x", b=2, x=GRID), ACT.Copy,
                           scale=mask_sb[of:of + 32, part:part + 1])
                else:
                    go(raw[:, 0:PAIR].rearrange("p (b n) -> p b n", b=2)[:, :, 1:NTOK],
                       bank.rearrange("p (b n) -> p b n", b=2), ACT.Identity, bias=conv_bias[:, 0:1]
                       ).then_inc(conv_read, 1)

            def attention(u, v, v_conv):
                if u == 6:
                    act.wait_ge(xn1_t, v)
                    go(xT1[:, 0:PAIR], A[:, 2, 0:PAIR], ACT.Copy).then_inc(xT1_ready, 1)
                if u in (7, 8):
                    n = 2 * (u - 7) + 1
                    act.wait_ge(qk_done[n], v)
                    for r in range(4):
                        last = go(k_sb[32 * r:32 * r + 32, n // 2, r, :],
                                  A[32 * r:32 * r + 32, (3 + n) % 4, 0:PAIR], ACT.Copy)
                    last.then_inc(qk_ready[n], 1)
                if u == 9:
                    act.wait_ge(v_done, v)
                    go(v_sb[:, :, :, 0:HD], A[0:T, 3, :].rearrange("p (j h d) -> p j h d", j=4, h=HEADS), ACT.Copy
                       ).then_inc(v_ready, 1)
                if 11 <= u < 19:
                    c = u - 11
                    act.wait_ge(pt_done[0][c], v)
                    go(probT[:, c % 2, 0], A[0:T, 2, 0:4 * T].rearrange("p (r q) -> p r q", r=4), ACT.Copy
                       ).then_inc(pt_ready[0][c], 1)
                if 10 <= u < 18:
                    c = u - 10
                    b, g, half = combo(c)
                    act.wait_ge(max_ready[c], v)
                    if c:
                        act.wait_ge(pt_done[1][c - 1], v)
                    for r in range(4):
                        last = go(prob[:, r, 0:NTOK], SCORES[:, r // 2, r % 2], ACT.Exp,
                                  bias=negmax[:, c, r:r + 1],
                                  accum_out=sums[:, 2 * b + half, 4 * g + r:4 * g + r + 1])
                    last.then_inc(exp_done[c], 1)
                if u == 24:
                    act.wait_ge(xn2_t, v)
                    go(xT2[:, 0:PAIR], A[:, 1, 0:PAIR], ACT.Copy).then_inc(xT2_ready, 1)
                if u == 26:
                    act.wait_ge(shifted_ready, v)
                    go(expl[:], shifted[:, :, 0:EXPERTS], ACT.Exp).then_inc(expl_ready, 1)
                if 29 <= u < 32 and v_conv is not None:
                    patches(u - 29, v_conv)

            def expert(i, n2):
                act.wait_ge(gate_done, n2)
                go(tanh[:, i % 2, :], gate_ps[:, 0:PAIR], ACT.Tanh, scale=0.5).then_inc(tanh_done, 1)

            def hand_over(v, units):
                act.wait_ge(up_done, units)
                act.wait_ge(xT2_ready, v)
                go(x_hi[:], xT2[:, 0:PAIR], ACT.Copy).then_inc(x_hi_ready, 1)
                act.wait_ge(share_t, v)
                go(share_sb[:], A[:, 3, 0:PAIR], ACT.Copy).then_inc(share_sb_ready, 1)

            def read_y(v):
                act.wait_ge(y_done, v)
                go(y_sb[:, 0:PAIR], y_ps[:, 0:PAIR], ACT.Copy).then_inc(y_read, 1)

            act.wait_ge(consts_in, 16 * 15)
            act.wait_ge(presets, 5)
            act.sem_inc(tanh_done, 1)
            for part in range(3):
                patches(part, 1)
            for u in range(UNITS):
                attention(u, 1, 2)
            hand_over(1, 1)

            def experts_and_attention(base, v, v_next, v_conv):
                for i in range(UNITS):
                    expert(i, base + (i + 2))
                    attention(i, v_next, v_conv)
                hand_over(v_next, base + (UNITS + 1))
                read_y(v)

            with act.Fori(0, PAIRS - 2) as p:
                experts_and_attention(act.snap(p * UNITS), act.snap(p + 1), act.snap(p + 2), act.snap(p + 3))
            experts_and_attention((PAIRS - 2) * UNITS, PAIRS - 1, PAIRS, None)
            for i in range(UNITS):
                expert(i, (PAIRS - 1) * UNITS + i + 2)
            read_y(PAIRS)

        @block.vector
        def _(dve):
            V = nc.vector

            def statistics(k, src, v):
                for j in range(4):
                    last = V.bn_stats(bn[:, k, j, :], src[:, j, :])
                last.then_inc(bn_done[k], 1)
                hold(dve, bn_done[k], v)
                for j in range(4):
                    last = V.bn_aggr(mv[:, k, j, :], bn[:, k, j, :])
                last.then_inc(var_ready[k], 1)

            def normalise(k, dst, src, v):
                dve.wait_ge(rstd_ready[k], v)
                for j in range(4):
                    last = V.tensor_scalar(dst[:, j, :], src[:, j, :], mv[:, k, j, 0:1], rstd[:, k, j:j + 1],
                                           ALU.subtract, ALU.mult)
                return last

            def attention(u, v, route):
                tok = A[0:T, 1, :].rearrange("p (j d) -> p j d", j=4)
                if u == 1:
                    dve.wait_ge(raw_t, v)
                    statistics(0, tok, v)
                if u == 2:
                    normalise(0, xn, tok, v).then_inc(z_ready, 1)
                if u == 4:
                    dve.wait_ge(h0_ready, v)
                    statistics(1, h0, v)
                if u == 5:
                    normalise(1, xn, h0, v).then_inc(xn1_ready, 1)
                if u in (7, 8):
                    n = 2 * (u - 7)
                    dve.wait_ge(qk_done[n], v)
                    V.tensor_scalar(q_sb[:, n // 2, 0:PAIR], A[:, (3 + n) % 4, 0:PAIR], HD ** -0.5, None, ALU.mult
                                    ).then_inc(qk_ready[n], 1)
                if 10 <= u < 18:
                    c = u - 10
                    dve.wait_ge(scores_done[c], v)
                    V.tensor_reduce(negmax[:, c, :].rearrange("p (a h) -> p a h", a=2), SCORES, AX_X, ALU.max,
                                    negate=True).then_inc(max_ready[c], 1)
                if 11 <= u < 19:
                    c = u - 11
                    dve.wait_ge(pt_done[1][c], v)
                    V.tensor_copy(probT[:, c % 2, 1], A[0:T, 2, 0:4 * T].rearrange("p (r q) -> p r q", r=4)
                                  ).then_inc(pt_ready[1][c], 1)
                if 12 <= u < 20:
                    c = u - 12
                    b, g, half = combo(c)
                    j = 2 * b + half
                    dve.wait_ge(pv_done[c], v)
                    V.tensor_copy(heads[:, g, START[j]:START[j] + WIDTH[j]], A[:, 3, 0:WIDTH[j]]
                                  ).then_inc(pv_read[c], 1)
                if u == 18:
                    dve.wait_ge(exp_done[7], v)
                    V.reciprocal(rinv[:], sums[:]).then_inc(rinv_done, 1)
                if u == 19:
                    dve.wait_ge(rinv_done, v)
                    dve.wait_ge(out_free, v)
                    for g in range(2):
                        for j in range(4):
                            last = V.tensor_copy(rwide[g][:, j, :].rearrange("p (r d) -> p r d", r=4),
                                                 rinv[:, j, 4 * g:4 * g + 4].unsqueeze(2).to_broadcast([T, 4, 32]))
                    last.then_inc(rwide_ready, 1)
                if u == 20:
                    dve.wait_ge(rwide_t, v)
                    dve.wait_ge(pv_read[7], v)
                    for g in range(2):
                        last = V.tensor_tensor(heads[:, g, 0:PAIR], heads[:, g, 0:PAIR], A[:, g, 0:PAIR], ALU.mult)
                    last.then_inc(heads_ready, 1)
                if u == 21:
                    dve.wait_ge(proj_done, v)
                    dve.wait_ge(h0_biased, v)
                    dve.wait_ge(resid_copied, v)
                    V.tensor_tensor(h1[:].rearrange("p j d -> p (j d)"), A[0:T, 2, :],
                                    h0[:].rearrange("p j d -> p (j d)"), ALU.add).then_inc(h1_ready, 1)
                if u == 22:
                    dve.wait_ge(h1_ready, v)
                    statistics(2, h1, v)
                if u == 23:
                    normalise(2, xn, h1, v).then_inc(xn2_ready, 1)
                if u == 25:
                    dve.wait_ge(logits_done, v)
                    V.tensor_tensor(logit[:], A[0:T, 3, 0:4 * EXPERTS].rearrange("p (j e) -> p j e", j=4),
                                    brout_sb[:].unsqueeze(1).to_broadcast([T, 4, EXPERTS]),
                                    ALU.add).then_inc(route_step, 1)
                    dve.wait_ge(route_step, route + 1)
                    V.tensor_reduce(lmax[:], logit[:], AX_X, ALU.max).then_inc(route_step, 1)
                    dve.wait_ge(route_step, route + 2)
                    V.tensor_tensor(logit[:], logit[:], lmax[:].unsqueeze(2).to_broadcast([T, 4, EXPERTS]),
                                    ALU.subtract).then_inc(route_step, 1)
                    dve.wait_ge(route_step, route + 3)
                    V.tensor_scalar(shifted[:, :, 0:EXPERTS], logit[:], LOWEST, None, ALU.max
                                    ).then_inc(shifted_ready, 1)
                if u == 26:
                    hold(dve, shifted_ready, v)
                    for j in range(4):
                        last = V.max(top8[:, j, :], shifted[:, j, 0:EXPERTS])
                    last.then_inc(route_step, 1)
                    dve.wait_ge(route_step, route + 4)
                    V.tensor_copy(topr[:, :, 0:TOPK], top8[:, :, 0:TOPK]).then_inc(route_step, 1)
                    hold(dve, route_step, route + 5)
                    for j in range(4):
                        last = V.match_replace(marked[:, j, :], topr[:, j, :], shifted[:, j, :], CHOSEN)
                    last.then_inc(route_step, 1)
                if u == 27:
                    dve.wait_ge(route_step, route + 6)
                    V.tensor_scalar(chosen[:], marked[:, :, 0:EXPERTS], CHOSEN, None, ALU.is_equal
                                    ).then_inc(chosen_ready, 1)
                    dve.wait_ge(expl_ready, v)
                    V.tensor_reduce(zsum[:, 0, :], expl[:], AX_X, ALU.add).then_inc(route_step, 1)
                    dve.wait_ge(route_step, route + 7)
                    V.scalar_tensor_tensor(expc[:], marked[:, :, 0:EXPERTS], CHOSEN, expl[:], ALU.is_equal, ALU.mult
                                           ).then_inc(route_step, 1)
                if u == 28:
                    dve.wait_ge(route_step, route + 8)
                    V.tensor_reduce(zsum[:, 1, :], expc[:], AX_X, ALU.add).then_inc(route_step, 1)
                    dve.wait_ge(route_step, route + 9)
                    V.scalar_tensor_tensor(zsum[:, 2, :], zsum[:, 0, :], GATE_EPS, zsum[:, 1, :], ALU.mult, ALU.add
                                           ).then_inc(route_step, 1)
                    dve.wait_ge(route_step, route + 10)
                    V.reciprocal(rden[:], zsum[:, 2, :]).then_inc(rden_ready, 1)
                if u == 29:
                    dve.wait_ge(rank_done, v)
                    V.tensor_tensor(slot[:], A[0:T, 2, 0:4 * EXPERTS].rearrange("p (j e) -> p j e", j=4),
                                    counts[:].unsqueeze(1).to_broadcast([T, 4, EXPERTS]), ALU.add
                                    ).then_inc(route_step, 1)
                    dve.wait_ge(route_step, route + 11)
                    V.tensor_tensor(counts[:], A[0:T, 2, 4 * EXPERTS:5 * EXPERTS], counts[:], ALU.add)
                    V.scalar_tensor_tensor(kept, slot[:], CAPACITY, expc[:], ALU.is_lt, ALU.mult
                                           ).then_inc(route_step, 1)
                    dve.wait_ge(route_step, route + 12)
                    dve.wait_ge(rden_ready, v)
                    V.tensor_tensor(slot[:], kept, rden[:].unsqueeze(2).to_broadcast([T, 4, EXPERTS]), ALU.mult
                                    ).then_inc(route_step, 1)
                if u == 30:
                    dve.wait_ge(route_step, route + 13)
                    V.tensor_copy(share_tok[:, :, 0:EXPERTS], slot[:]).then_inc(share_hi, 1)
                    dve.wait_ge(share_hi, v)
                    V.tensor_tensor(share_tok[:, :, EXPERTS:], slot[:], share_tok[:, :, 0:EXPERTS].bitcast(F32),
                                    ALU.subtract).then_inc(share_tok_ready, 1)

            def expert(i, n2):
                h = hidden[:, i % 3, :]
                dve.wait_ge(tanh_done, n2)
                V.scalar_tensor_tensor(h, tanh[:, i % 2, :], 1.0, gate_ps[:, 0:PAIR], ALU.add, ALU.mult
                                       ).then_inc(silu_done, 1)
                dve.wait_ge(silu_done, n2)
                dve.wait_ge(up_done, n2)
                V.tensor_tensor(h, h, up_ps[:, 0:PAIR], ALU.mult).then_inc(gated_done, 1)
                dve.wait_ge(gated_done, n2)
                if i < ROUTED:
                    dve.wait_ge(share_done, n2)
                    V.tensor_tensor(h, h, share_ps[:, 0:PAIR], ALU.mult).then_inc(hidden_done, 1)
                else:
                    V.tensor_scalar(h, h, 0.25, None, ALU.mult).then_inc(hidden_done, 1)

            def add_output(v):
                dve.wait_ge(y_t, v)
                dve.wait_ge(resid_copied, v + 1)
                dve.wait_ge(out_free, v + 1)
                V.tensor_tensor(out_sb[:].rearrange("p j d -> p (j d)"), A[0:T, 2, :],
                                resid[:].rearrange("p j d -> p (j d)"), ALU.add).then_inc(out_added, 1)

            for t in (raw[:], pad_y[:], pad_x[:], xT1[:], q_sb[:], k_sb[:], v_sb[:], prob[:], heads[:], xT2[:], counts[:]):
                V.memset(t, 0.0)
            V.memset(topr[:], FILLER)
            V.memset(shifted[:], FILLER)
            V.memset(half_neg[:], -0.5).then_inc(presets, 4)
            dve.sem_inc(silu_done, 1)
            dve.sem_inc(gated_done, 1)
            dve.sem_inc(hidden_done, 1)
            dve.sem_inc(gate_done, 1)
            dve.sem_inc(up_done, 1)
            dve.sem_inc(share_done, 1)
            dve.sem_inc(out_added, CREDITS_Y)
            dve.sem_inc(out_free, CREDITS_Y)
            dve.sem_inc(resid_copied, 1)
            dve.wait_ge(consts_in, 16 * 15)
            V.tensor_copy(before_sb[:], before_f).then_inc(presets, 1)
            dve.wait_ge(presets, 5)
            for n, (hi, lo) in enumerate(((gate_hi, gate_lo), (up_hi, up_lo))):
                flat = hi[:].rearrange("p u m -> p (u m)")
                dve.wait_ge(stage_in, 16 * (n + 1))
                V.tensor_copy(flat, stage).then_inc(split_step, 1)
                dve.wait_ge(split_step, 2 * n + 1)
                V.tensor_tensor(lo[:].rearrange("p u m -> p (u m)"), stage, flat.bitcast(F32), ALU.subtract
                                ).then_inc(split_step, 1)
            dve.wait_ge(stage_in, 48)
            V.tensor_copy(select_sb[:].rearrange("p u m -> p (u m)"), stage[:, 0:ROUTED * 128]).then_inc(split_step, 1)

            for u in range(UNITS):
                attention(u, 1, 0)

            def experts_and_attention(base, v, v_next, route):
                for i in range(UNITS):
                    expert(i, base + (i + 2))
                    attention(i, v_next, route)
                add_output(v)

            with dve.Fori(0, PAIRS - 2) as p:
                experts_and_attention(dve.snap(p * UNITS), dve.snap(p + 1), dve.snap(p + 2),
                                      dve.snap(ROUTE_STEPS * (p + 1)))
            experts_and_attention((PAIRS - 2) * UNITS, PAIRS - 1, PAIRS, ROUTE_STEPS * (PAIRS - 1))
            for i in range(UNITS):
                expert(i, (PAIRS - 1) * UNITS + i + 2)
            add_output(PAIRS)

        @block.gpsimd
        def _(pool):
            G = nc.gpsimd

            def root(k, v):
                hold(pool, var_ready[k], v)
                G.tensor_scalar(var_eps[:, k, :], mv[:, k, :, 1], EPS, None, ALU.add).then_inc(eps_added[k], 1)
                pool.wait_ge(eps_added[k], v)
                G.tensor_tensor(rstd[:, k, :], var_eps[:, k, :], half_neg[:], ALU.pow).then_inc(rstd_ready[k], 1)

            def neighbours(v):
                pool.wait_ge(conv_read, v)
                for pad, sem_, places in ((pad_y, raw_step, ((64, 2, 1), (96, 0, 1))),
                                          (pad_x, raw_ready, ((64, 1, 2), (96, 1, 0)))):
                    for at, dy, dx in places:
                        dst = raw[at:at + 32, 0:PAIR].rearrange("p (b n) -> p b n", b=2)[:, :, 1:NTOK].rearrange(
                            "p b (t x) -> p b t x", x=GRID)
                        last = G.tensor_tensor(dst, dst, pad[at:at + 32, :, dy:dy + GRID, dx:dx + GRID], ALU.add)
                    last.then_inc(sem_, 1)
                    pool.wait_ge(sem_, v)

            def attention(u, v, v_conv):
                if u == 1:
                    root(0, v)
                if u == 2:
                    pool.wait_ge(z_ready, v)
                    G.tensor_tensor(xn[:], xn[:], lng_sb[:].unsqueeze(1).to_broadcast([T, 4, 128]), ALU.mult
                                    ).then_inc(scaled, 1)
                    pool.wait_ge(scaled, v)
                    G.tensor_tensor(h0[:], xn[:], lnb_sb[:].unsqueeze(1).to_broadcast([T, 4, 128]), ALU.add).then_inc(shifted_h0, 1)
                    hold(pool, shifted_h0, v)
                    G.tensor_copy(h0[0:1, 2, :], cls_sb[:])
                    G.tensor_copy(h0[0:1, 0, :], cls_sb[:]).then_inc(h0_ready, 1)
                if u == 4:
                    root(1, v)
                if u == 5:
                    pool.wait_ge(xn1_ready, v)
                    G.tensor_tensor(h0[:], h0[:], bproj_sb[:].unsqueeze(1).to_broadcast([T, 4, 128]), ALU.add).then_inc(h0_biased, 1)
                if u == 22:
                    root(2, v)
                if u == 31 and v_conv is not None:
                    pool.wait_ge(rstd_ready[2], v)
                    neighbours(v_conv)

            def hand_over(v):
                pool.wait_ge(x_hi_ready, v)
                G.tensor_tensor(x_lo[:], xT2[:, 0:PAIR], x_hi[:].bitcast(F32), ALU.subtract).then_inc(x_lo_ready, 1)
                pool.wait_ge(h1_ready, v)
                hold(pool, out_added, v + 1)
                G.tensor_copy(resid[:], h1[:]).then_inc(resid_copied, 1)

            pool.wait_ge(consts_in, 16 * 15)
            pool.wait_ge(presets, 5)
            neighbours(1)
            for u in range(UNITS):
                attention(u, 1, 2)
            hand_over(1)
            with pool.Fori(0, PAIRS - 2) as p:
                v_next, v_conv = pool.snap(p + 2), pool.snap(p + 3)
                for i in range(UNITS):
                    attention(i, v_next, v_conv)
                hand_over(v_next)
            for i in range(UNITS):
                attention(i, PAIRS, None)
            hand_over(PAIRS)


def kernel(**inputs):
    import numpy as np
    import concourse.bacc as bacc
    from concourse.bass_utils import run_bass_kernel_spmd as run

    a = {k: np.asarray(v) for k, v in inputs.items()}
    f4 = np.float32
    P = PS

    main = a["L0_tok_W_main"].reshape(64, 3, P, 2, HP).transpose(3, 1, 2, 4, 0)
    sy = a["L0_tok_W_sy"].reshape(16, 3, P, 2, HP).transpose(3, 1, 2, 4, 0)
    sx = a["L0_tok_W_sx"].reshape(16, 3, P, 2, HP).transpose(3, 1, 2, 4, 0)
    conv = np.zeros((2, 3, P, HP, 128), f4)
    conv[..., 0:64] = main
    conv[:, :, HP:, :, 64:80] = sy[:, :, :HP]
    conv[1, ..., 80:96] = sx[0]
    conv[:, :, :HP, :, 96:112] = sy[:, :, HP:]
    conv[0, ..., 112:128] = sx[1]
    bm, bx, by = a["L0_tok_b_main"], a["L0_tok_b_sx"], a["L0_tok_b_sy"]
    conv_b = np.concatenate([bm, by, bx, by, bx]).reshape(128, 1)
    masks = np.zeros((4, 2, 16, 2), f4)
    masks[:, 0, :, 0] = 1
    masks[:, 1, :, 1] = 1
    perm = np.zeros((128, 128), f4)
    order = np.concatenate([np.arange(64), np.arange(96, 112), np.arange(64, 80), np.arange(112, 128),
                            np.arange(80, 96)])
    perm[np.arange(128), order] = 1

    qkv = a["L0_attn_w_qkv"].reshape(3, 2, 4, HD, D)
    w_qk = np.zeros((D, 2, 2, 4, 32), f4)
    w_qk[..., 0:HD] = qkv[0:2].transpose(4, 1, 0, 2, 3)
    w_p = np.zeros((2, 4, 32, D), f4)
    w_p[:, :, 0:HD, :] = a["L0_attn_w_proj"].T.reshape(2, 4, HD, D)

    def by_feature(routed, shared):
        return np.concatenate([routed.reshape(-1, D), shared.reshape(-1, D)]).T

    down = np.concatenate([a["L0_ffn_w_down"], a["L0_ffn_shared_w_down"]]).transpose(0, 2, 1)
    select = np.zeros((2, EXPERTS, EXPERTS, F), f4)
    select[:, np.arange(EXPERTS), np.arange(EXPERTS), :] = 0.5
    before = np.ones((T, 2, T), f4)
    before[:, 0, :] = np.triu(np.ones((T, T), f4), 1)

    arrays = {
        "x": a["x"], "conv_w": conv.reshape(96, HP * 128), "conv_b": conv_b, "masks": masks.reshape(128, 2),
        "perm": perm, "ident": np.eye(128, dtype=f4), "cls_tok": a["cls_tok"].reshape(1, D),
        "ln_g": np.broadcast_to(a["L0_tok_ln_g"], (T, D)), "ln_b": np.broadcast_to(a["L0_tok_ln_b"], (T, D)),
        "w_qk": w_qk.reshape(D, 512), "w_v": qkv[2].reshape(D, D).T,
        "w_p": w_p.reshape(2, 128, D).transpose(1, 0, 2).reshape(128, 256),
        "b_proj": np.broadcast_to(a["L0_attn_b_proj"], (T, D)),
        "w_r": a["L0_ffn_router_w"].T, "b_r": np.broadcast_to(a["L0_ffn_bias"], (T, EXPERTS)),
        "w_gate": by_feature(a["L0_ffn_w_gate"], a["L0_ffn_shared_w_gate"]),
        "w_up": by_feature(a["L0_ffn_w_up"], a["L0_ffn_shared_w_up"]),
        "w_down": down.reshape(UNITS, 128, D).transpose(1, 0, 2).reshape(128, UNITS * D),
        "select": select.reshape(128, EXPERTS * F), "before": before.reshape(T, 2 * T),
    }
    arrays = {k: np.ascontiguousarray(v) for k, v in arrays.items()}
    nc = bacc.Bacc("TRN2", target_bir_lowering=False, num_devices=1)
    args = [nc.dram_tensor(f"in_{k}", v.shape, mybir.dt.from_np(v.dtype), kind="ExternalInput").ap()
            for k, v in arrays.items()]
    shape = (a["x"].shape[0], NTOK, D)
    args.append(nc.dram_tensor("out_0", shape, F32, kind="ExternalOutput").ap())
    vit_layer(nc, **dict(zip(list(arrays) + ["out"], args)))
    r = run(nc, [{f"in_{k}": v for k, v in arrays.items()}], core_ids=[0])
    return r.results[0]["out_0"]
```

```python
from contextlib import ExitStack

import concourse.bass as bass
from concourse import mybir

F32 = mybir.dt.float32
F32R = mybir.dt.float32r
BF16 = mybir.dt.bfloat16
ALU = mybir.AluOpType
ACT = mybir.ActivationFunctionType
AX_X = mybir.AxisListType.X

D = 128
HEADS, HD = 8, 16
PS, HP = 16, 8
GRID = 14
NTOK = 1 + GRID * GRID
PAIR = 2 * NTOK
COLS = PAIR + 2
T = 99
START = [0, T, NTOK, NTOK + T]
WIDTH = [T, NTOK - T, T, NTOK - T]
EXPERTS, TOPK, F = 64, 6, 64
ROUTED = EXPERTS // 2
UNITS = ROUTED + 1
EPS = 1e-5
GATE_EPS = 1e-9
LOWEST = -104.0
FILLER = -1e30
CHOSEN = 1.0
CREDITS_Y = 2
ROUTE_STEPS = 12
CONV_AT = {0: 2, 1: 2, 2: 2, 3: 2}
BY_POOL = list(range(6, ROUTED))
HALVES = 16
PRODUCT_LATE = range(9, 17)
STORE_AT, LOAD_AT = 8, 14
SLOTS = 8


def vit_layer(nc, x, conv_w, conv_b, masks, perm, ident, cls_tok, ln_g, ln_b, w_qk, w_v, w_p, b_proj,
              w_r, b_r, w_gate, w_up, w_down, before, out):
    B = x.shape[0]
    PAIRS = B // 2
    CAPACITY = float(max(1, int(B * NTOK * TOPK * 2.0 / EXPERTS)))

    with ExitStack() as ctx:
        def sb(name, shape, dt=F32):
            return ctx.enter_context(nc.sbuf_tensor(name, shape, dt))

        def sem(name):
            return ctx.enter_context(nc.semaphore(name))

        def sems(name, n):
            return [sem(f"{name}{i}") for i in range(n)]

        gate_ps = ctx.enter_context(nc.psum_tensor("gate_ps", [128, 2, 512], F32))
        up_ps = ctx.enter_context(nc.psum_tensor("up_ps", [128, 512], F32))
        y_ps = ctx.enter_context(nc.psum_tensor("y_ps", [128, 512], F32))
        A = ctx.enter_context(nc.psum_tensor("A", [128, 4, 512], F32))
        SCORES = A[0:T, 0:2, 0:PAIR].rearrange("p a (h k) -> p a h k", h=2)

        conv_sb = sb("conv_sb", [96, HP, 128])
        conv_bias = sb("conv_bias", [128, 1])
        mask_sb = sb("mask_sb", [128, 2])
        perm_sb = sb("perm_sb", [128, 128])
        id_sb = sb("id_sb", [128, 128])
        cls_sb = sb("cls_sb", [1, 128])
        lng_sb = sb("lng_sb", [T, 128])
        lnb_sb = sb("lnb_sb", [T, 128])
        bproj_sb = sb("bproj_sb", [T, 128])
        brout_sb = sb("brout_sb", [T, EXPERTS])
        wqk_sb = sb("wqk_sb", [128, 4, 128])
        wv_sb = sb("wv_sb", [128, 128])
        wp_sb = sb("wp_sb", [128, 2, 128])
        wr_sb = sb("wr_sb", [128, EXPERTS])
        before_sb = sb("before_sb", [T, 2, T], BF16)
        half_neg = sb("half_neg", [T, 4])
        gate_hi = sb("gate_hi", [128, UNITS, 128], F32R)
        gate_lo = sb("gate_lo", [128, UNITS, 128], F32R)
        up_hi = sb("up_hi", [128, UNITS, 128], F32R)
        up_lo = sb("up_lo", [128, UNITS, 128], F32R)
        down_sb = sb("down_sb", [128, UNITS, 128])
        stage = down_sb[:].rearrange("p u m -> p (u m)")


        image = sb("image", [96, 2 * GRID, GRID * PS])
        raw = sb("raw", [128, COLS])
        pad_y = sb("pad_y", [128, 2, 16, 16])
        pad_x = sb("pad_x", [128, 2, 16, 16])
        bn = sb("bn", [T, 3, 4, 6])
        mv = sb("mv", [T, 3, 4, 2])
        var_eps = sb("var_eps", [T, 3, 4])
        rstd = sb("rstd", [T, 3, 4])
        h0 = sb("h0", [T, 4, 128])
        xn = sb("xn", [T, 4, 128])
        xT1 = sb("xT1", [128, COLS])
        q_sb = sb("q_sb", [128, 2, COLS])
        k_sb = sb("k_sb", [128, 2, 4, PAIR])
        v_sb = sb("v_sb", [T, 4, HEADS, 32])
        negmax = sb("negmax", [T, 8, 4])
        sums = sb("sums", [T, 4, HEADS])
        rinv = sb("rinv", [T, 4, HEADS])
        out_sb = sb("out_sb", [T, 4, 128])
        rwide = [xn, out_sb]
        prob = sb("prob", [T, 2, 4, NTOK + 1])
        probT = sb("probT", [T, 2, 2, 4, T])
        heads = sb("heads", [128, 2, COLS])
        h1 = sb("h1", [T, 4, 128])
        before_f = h1[:].rearrange("p j d -> p (j d)")[:, 0:2 * T].rearrange("p (a b) -> p a b", a=2)
        resid = sb("resid", [T, 4, 128])
        xT2 = sb("xT2", [128, COLS])
        logit = sb("logit", [T, 4, EXPERTS])
        lmax = sb("lmax", [T, 4])
        shifted = sb("shifted", [T, 4, EXPERTS + 2])
        marked = sb("marked", [T, 4, EXPERTS + 2])
        top8 = sb("top8", [T, 4, 8])
        topr = sb("topr", [T, 4, 8])
        chosen = sb("chosen", [T, 4, EXPERTS], BF16)
        expl = sb("expl", [T, 4, EXPERTS])
        expc = expl
        zsum = sb("zsum", [T, 3, 4])
        rden = sb("rden", [T, 4])
        slot = logit
        share_tok = sb("share_tok", [T, 4, 128])
        kept = marked[:, :, 0:EXPERTS]
        counts = sb("counts", [T, EXPERTS])
        share_sb = sb("share_sb", [EXPERTS, PAIR])
        spread = sb("spread", [128, SLOTS, PAIR])
        x_hi = sb("x_hi", [128, PAIR], F32R)
        x_lo = sb("x_lo", [128, PAIR], F32R)
        tanh = sb("tanh", [128, 2, PAIR])
        hidden = sb("hidden", [128, 3, PAIR])
        y_sb = heads[:, 0, :]

        consts_in = sem("consts_in")
        weights_in = sem("weights_in")
        stage_in = sem("stage_in")
        split_step = sem("split_step")
        presets = sem("presets")
        image_in = sem("image_in")
        conv_done = sem("conv_done")
        conv_read = sem("conv_read")
        raw_step = sem("raw_step")
        raw_ready = sem("raw_ready")
        raw_t = sem("raw_t")
        bn_done = sems("bn_done", 3)
        var_ready = sems("var_ready", 3)
        eps_added = sems("eps_added", 3)
        rstd_ready = sems("rstd_ready", 3)
        z_ready = sem("z_ready")
        scaled = sem("scaled")
        shifted_h0 = sem("shifted_h0")
        h0_ready = sem("h0_ready")
        h0_biased = sem("h0_biased")
        xn1_ready = sem("xn1_ready")
        xn1_t = sem("xn1_t")
        xT1_ready = sem("xT1_ready")
        qk_done = sems("qk_done", 4)
        qk_ready = sems("qk_ready", 4)
        v_done = sem("v_done")
        v_ready = sem("v_ready")
        score_halves = sem("score_halves")
        max_halves = sem("max_halves")
        exp_halves = sem("exp_halves")
        pt_done = [sems("pt_done_a", 8), sems("pt_done_b", 8)]
        pt_ready = [sems("pt_ready_a", 8), sems("pt_ready_b", 8)]
        pv_done = sems("pv_done", 8)
        pv_read = sems("pv_read", 8)
        rinv_done = sem("rinv_done")
        rwide_ready = sem("rwide_ready")
        rwide_t = sem("rwide_t")
        heads_ready = sem("heads_ready")
        proj_done = sem("proj_done")
        h1_ready = sem("h1_ready")
        xn2_ready = sem("xn2_ready")
        xn2_t = sem("xn2_t")
        xT2_ready = sem("xT2_ready")
        logits_done = sem("logits_done")
        route_step = sem("route_step")
        shifted_ready = sem("shifted_ready")
        chosen_ready = sem("chosen_ready")
        expl_ready = sem("expl_ready")
        rden_ready = sem("rden_ready")
        rank_done = sem("rank_done")

        share_tok_ready = sem("share_tok_ready")
        share_t = sem("share_t")
        share_sb_ready = sem("share_sb_ready")
        spread_in = sems("spread_in", SLOTS)
        x_hi_ready = sem("x_hi_ready")
        x_lo_ready = sem("x_lo_ready")
        resid_copied = sem("resid_copied")
        gate_done = sem("gate_done")
        up_done = sem("up_done")

        tanh_done = sem("tanh_done")

        silu_done = sem("silu_done")
        gated_done = sem("gated_done")
        hidden_done = sem("hidden_done")
        y_done = sem("y_done")
        y_half_read = sem("y_half_read")
        y_read = sem("y_read")
        y_t = sem("y_t")
        out_added = sem("out_added")
        out_stored = sem("out_stored")
        out_free = sem("out_free")

        x_view = x.rearrange("(p b) c (t y) x -> p c y b t x", b=2, y=PS)
        out_view = out.rearrange("(p b) t d -> p t b d", b=2)
        IMAGE = 12 * 16
        FILLED = 2 * 16 * ROUTED // SLOTS
        STORED = 2 * 16

        def combo(c):
            return c // 4, c // 2 % 2, c % 2

        def hold(eng, sem_, value):
            eng.wait_ge(sem_, value)
            eng.nop(nofuse=True)

        block = ctx.enter_context(nc.Block())

        @block.sync
        def _(sp):
            for dst, src in ((conv_sb[:], conv_w.rearrange("p (a b) -> p a b", a=HP)),
                             (conv_bias[:], conv_b), (mask_sb[:], masks), (perm_sb[:], perm),
                             (id_sb[:], ident), (cls_sb[:], cls_tok),
                             (wqk_sb[:], w_qk.rearrange("p (a b) -> p a b", a=4)), (wv_sb[:], w_v),
                             (wp_sb[:], w_p.rearrange("p (a b) -> p a b", a=2)), (wr_sb[:], w_r),
                             (before_f, before.rearrange("p (a b) -> p a b", a=2))):
                sp.dma_start(dst, src).then_inc(consts_in, 16)

            def load_part(p, n):
                g, c, b = n // 6, n // 2 % 3, n % 2
                w = GRID * PS - HP * g
                sp.dma_start(image[48 * g + 16 * c:48 * g + 16 * c + 16, GRID * b:GRID * (b + 1), 0:w],
                             x_view[p, c, :, b, :, HP * g:HP * g + w]).then_inc(image_in, 16)

            def load_image(p):
                for n in range(12):
                    load_part(p, n)

            load_image(0)
            for dst, src in ((lng_sb, ln_g), (lnb_sb, ln_b), (bproj_sb, b_proj), (brout_sb, b_r)):
                sp.dma_start(dst[:], src).then_inc(consts_in, 16)
            sp.dma_start(stage, w_gate).then_inc(stage_in, 16)
            sp.wait_ge(conv_done, 1)
            load_image(1)
            sp.wait_ge(split_step, 2)
            sp.dma_start(stage, w_up).then_inc(stage_in, 16)
            sp.wait_ge(conv_done, 2)
            load_image(2)
            sp.wait_ge(split_step, 4)
            sp.dma_start(stage, w_down).then_inc(weights_in, 16)

            def store(p):
                sp.wait_ge(out_added, p + 1 + CREDITS_Y)
                for half in range(2):
                    w = WIDTH[half]
                    sp.dma_start(out_view[p, T * half:T * half + w],
                                 out_sb[0:w].rearrange("t (b h) d -> t h b d", h=2)[:, half]
                                 ).then_inc(out_stored, 16)
                sp.wait_ge(out_stored, STORED * (p + 1))
                sp.sem_inc(out_free, 1)

            def fill(k):
                for e in range(2):
                    sp.dma_start(spread[F * e:F * e + F, k % SLOTS, :],
                                 share_sb[2 * k + e:2 * k + e + 1, :].unsqueeze(1).to_broadcast([1, F, PAIR])
                                 ).then_inc(spread_in[k % SLOTS], 16)

            def serve(p, base, first, more):
                sp.wait_ge(share_sb_ready, p + 1)
                for k in range(ROUTED):
                    if k >= SLOTS:
                        sp.wait_ge(hidden_done, base + (k - SLOTS + 2))
                    elif not first:
                        sp.wait_ge(hidden_done, base + (k + ROUTED - SLOTS - UNITS + 2))
                    fill(k)
                    if k == STORE_AT and not first:
                        store(p - 1)
                    if k == LOAD_AT and more:
                        sp.wait_ge(conv_done, p + 3)
                    if LOAD_AT <= k < LOAD_AT + 12 and more:
                        load_part(p + 3, k - LOAD_AT)

            serve(0, 0, True, True)
            with sp.Fori(0, PAIRS - 4) as n:
                serve(sp.snap(n + 1), sp.snap((n + 1) * UNITS), False, True)
            for p in range(PAIRS - 3, PAIRS):
                serve(p, p * UNITS, False, False)
            store(PAIRS - 1)

        @block.tensor
        def _(pe):
            mm, tr = nc.tensor.matmul, nc.tensor.transpose
            ident_t = id_sb[0:T, 0:T]

            def conv(lo, hi):
                for px in range(lo, hi):
                    last = mm(A[:, 0, 0:2 * GRID * GRID].rearrange("p (t x) -> p t x", x=GRID),
                              conv_sb[:, px, :],
                              image[:].rearrange("p t (x q) -> p t x q", q=PS)[:, :, :, px],
                              start=(px == 0), stop=(px == HP - 1))
                return last

            def tokens_to_features(dst, src):
                for j in range(4):
                    w = WIDTH[j]
                    last = tr(dst[:, START[j]:START[j] + w], src[0:w, j, :], id_sb[0:w, 0:w])
                return last

            def scores(c, h):
                b, g, half = combo(c)
                j = 2 * b + half
                for r in (2 * h, 2 * h + 1):
                    last = mm(SCORES[:, h, r % 2], q_sb[:, g, START[j]:START[j] + T],
                              k_sb[:, g, r, NTOK * b:NTOK * (b + 1)], start=True, stop=True)
                last.then_inc(score_halves, 1)

            def transpose_probs(c, kt, lo, hi):
                for r in range(lo, hi):
                    last = tr(A[0:T, 2, T * r:T * (r + 1)], prob[:, c % 2, r, T * kt:T * kt + T], ident_t)
                if hi == 4:
                    last.then_inc(pt_done[kt][c], 1)

            def weigh_values(c):
                b, g, half = combo(c)
                for r in range(4):
                    for kt in range(2):
                        w = WIDTH[kt]
                        last = mm(A[32 * r:32 * r + 32, 3, 0:T],
                                  v_sb[0:w, 2 * b + kt, 4 * g + r, :], probT[0:w, c % 2, kt, r, :],
                                  start=(kt == 0), stop=(kt == 1), tile_position=(0, 32 * r))
                last.then_inc(pv_done[c], 1)

            def conv_part(u, pixels):
                if u in CONV_AT:
                    lo = sum(n for at, n in CONV_AT.items() if at < u)
                    if lo == 0:
                        pe.wait_ge(image_in, pixels)
                    last = conv(lo, lo + CONV_AT[u])
                    if lo + CONV_AT[u] == HP:
                        last.then_inc(conv_done, 1)

            def values(c, v):
                if c == 0:
                    pe.wait_ge(v_ready, v)
                pe.wait_ge(pt_ready[1][c], v)
                if c:
                    pe.wait_ge(pv_read[c - 1], v)
                weigh_values(c)

            def attention_input(v):
                pe.wait_ge(xn1_ready, v)
                pe.wait_ge(out_added, v)
                tokens_to_features(A[:, 2, :], xn).then_inc(xn1_t, 1)

            def attention(u, v, halves, v_conv, last_product):
                if u == 0:
                    pe.wait_ge(raw_ready, v)
                    for j in range(4):
                        last = tr(A[0:T, 1, 128 * j:128 * j + 128], raw[:, START[j]:START[j] + T], perm_sb[:])
                    last.then_inc(raw_t, 1)
                if u in (6, 7):
                    if u == 6:
                        pe.wait_ge(xT1_ready, v)
                        if v_conv is not None:
                            pe.wait_ge(conv_read, v_conv)
                    for n in (2 * (u - 6), 2 * (u - 6) + 1):
                        mm(A[:, (3 + n) % 4, 0:PAIR], wqk_sb[:, n, :], xT1[:, 0:PAIR],
                           start=True, stop=True).then_inc(qk_done[n], 1)
                if u == 8:
                    pe.wait_ge(qk_ready[0], v)
                    for j in range(4):
                        last = mm(A[0:T, 3, 128 * j:128 * j + 128], xT1[:, START[j]:START[j] + T], wv_sb[:],
                                  start=True, stop=True)
                    last.then_inc(v_done, 1)
                    for n in range(4):
                        pe.wait_ge(qk_ready[n], v)
                if 8 <= u < 17:
                    c = u - 8
                    for h in range(2):
                        if c == 8 and h == 1:
                            values(6, v)
                        if c:
                            pe.wait_ge(exp_halves, halves + (2 * c - 1 + h))
                        if c < 8:
                            scores(c, h)
                        if c > 1 and h == 0:
                            pe.wait_ge(pt_ready[1][c - 2], v)
                        if c:
                            transpose_probs(c - 1, 0, 2 * h, 2 * h + 2)
                    if 1 < c < 8:
                        values(c - 2, v)
                    if c:
                        last_product()
                        pe.wait_ge(pt_ready[0][c - 1], v)
                        transpose_probs(c - 1, 1, 0, 4)
                if u == 17:
                    values(7, v)
                if u == 18:
                    pe.wait_ge(rwide_ready, v)
                    for g in range(2):
                        last = tokens_to_features(A[:, g, :], rwide[g])
                    last.then_inc(rwide_t, 1)
                if u == 19:
                    pe.wait_ge(heads_ready, v)
                    for j in range(4):
                        for g in range(2):
                            last = mm(A[0:T, 2, 128 * j:128 * j + 128], heads[:, g, START[j]:START[j] + T],
                                      wp_sb[:, g, :], start=(g == 0), stop=(g == 1))
                    last.then_inc(proj_done, 1)
                if u == 23:
                    pe.wait_ge(xn2_ready, v)
                    tokens_to_features(A[:, 1, :], xn).then_inc(xn2_t, 1)
                if u == 24:
                    pe.wait_ge(xT2_ready, v)
                    for j in range(4):
                        last = mm(A[0:T, 3, EXPERTS * j:EXPERTS * (j + 1)], xT2[:, START[j]:START[j] + T], wr_sb[:],
                                  start=True, stop=True)
                    last.then_inc(logits_done, 1)
                if u == 29:
                    pe.wait_ge(chosen_ready, v)
                    for j in range(5):
                        for i in range(min(j, 3) + 1):
                            kind = 0 if i == j else 1
                            last = mm(A[0:T, 2, EXPERTS * j:EXPERTS * (j + 1)], before_sb[0:WIDTH[i], kind, :],
                                      chosen[0:WIDTH[i], i, :], start=(i == 0), stop=(i == min(j, 3)))
                    last.then_inc(rank_done, 1)
                if u == 32:
                    pe.wait_ge(share_tok_ready, v)
                    tokens_to_features(A[:, 3, :], share_tok).then_inc(share_t, 1)

            def expert_in(i, n0, n1, v, between):
                if i == 0:
                    pe.wait_ge(x_lo_ready, v)
                if i != 1:
                    pe.wait_ge(silu_done, n1 if i == 0 else n0)
                for w, xs, s, e in ((gate_hi, x_lo, True, False), (gate_lo, x_hi, False, False),
                                    (gate_hi, x_hi, False, True)):
                    last = mm(gate_ps[:, i % 2, 0:PAIR], w[:, i, :], xs[:], start=s, stop=e)
                last.then_inc(gate_done, 1)
                between()
                pe.wait_ge(gated_done, n1)
                for w, xs, s, e in ((up_hi, x_lo, True, False), (up_lo, x_hi, False, False),
                                    (up_hi, x_hi, False, True)):
                    last = mm(up_ps[:, 0:PAIR], w[:, i, :], xs[:], start=s, stop=e)
                last.then_inc(up_done, 1)

            def expert_out(i, base):
                pe.wait_ge(hidden_done, base + (i + 2))
                last = mm(y_ps[:, 0:PAIR], down_sb[:, i, :], hidden[:, i % 3, :],
                          start=(i == 0), stop=(i == UNITS - 1))
                if i == UNITS - 1:
                    last.then_inc(y_done, 1)

            def experts_and_attention(v, base, v_next, halves, v_conv, pixels):
                for i in range(UNITS):
                    def last_product():
                        if i >= 2:
                            expert_out(i - 2, base)

                    def between():
                        if v_next is None or i not in PRODUCT_LATE:
                            last_product()
                        if v_next is not None and i == 6:
                            attention_input(v_next)

                    expert_in(i, base + i, base + (i + 1), v, between)
                    if v_next is not None:
                        attention(i, v_next, halves, v_conv, last_product)
                    if pixels is not None:
                        conv_part(i, pixels)
                expert_out(UNITS - 2, base)
                expert_out(UNITS - 1, base)
                pe.wait_ge(y_half_read, v)
                for j in range(4):
                    if j == 2:
                        pe.wait_ge(y_read, v)
                    last = tr(A[0:T, 2, 128 * j:128 * j + 128], y_sb[:, START[j]:START[j] + T], id_sb[:])
                last.then_inc(y_t, 1)

            pe.wait_ge(consts_in, 16 * 15)
            pe.wait_ge(presets, 5)
            pe.wait_ge(image_in, IMAGE)
            conv(0, HP).then_inc(conv_done, 1)
            for u in range(UNITS):
                if u == 6:
                    attention_input(1)
                attention(u, 1, 0, 2, lambda: None)
                conv_part(u, 2 * IMAGE)
            pe.wait_ge(weights_in, 16)
            pe.wait_ge(split_step, 4)
            with pe.Fori(0, PAIRS - 2) as p:
                experts_and_attention(pe.snap(p + 1), pe.snap(p * UNITS), pe.snap(p + 2), pe.snap(HALVES * (p + 1)),
                                      pe.snap(p + 3), IMAGE * (p + 3))
            experts_and_attention(PAIRS - 1, (PAIRS - 2) * UNITS, PAIRS, HALVES * (PAIRS - 1), None, None)
            experts_and_attention(PAIRS, (PAIRS - 1) * UNITS, None, None, None, None)

        @block.scalar
        def _(act):
            go = nc.scalar.activation

            def patches(part, v):
                bank = A[:, 0, 0:2 * GRID * GRID]
                if part == 0:
                    act.wait_ge(conv_done, v)
                if part < 2:
                    pad = (pad_y, pad_x)[part]
                    for to, of in ((64, 96), (96, 64)):
                        go(pad[to:to + 32, :, 1:1 + GRID, 1:1 + GRID],
                           bank[of:of + 32].rearrange("p (b t x) -> p b t x", b=2, x=GRID), ACT.Copy,
                           scale=mask_sb[of:of + 32, part:part + 1])
                else:
                    go(raw[:, 0:PAIR].rearrange("p (b n) -> p b n", b=2)[:, :, 1:NTOK],
                       bank.rearrange("p (b n) -> p b n", b=2), ACT.Identity, bias=conv_bias[:, 0:1]
                       ).then_inc(conv_read, 1)

            def exponentials(c, h, halves):
                b, g, half = combo(c)
                act.wait_ge(max_halves, halves + (2 * c + h + 1))
                for r in (2 * h, 2 * h + 1):
                    last = go(prob[:, c % 2, r, 0:NTOK], SCORES[:, h, r % 2], ACT.Exp,
                              bias=negmax[:, c, r:r + 1],
                              accum_out=sums[:, 2 * b + half, 4 * g + r:4 * g + r + 1])
                last.then_inc(exp_halves, 1)

            def attention(u, v, halves, v_conv):
                if u == 3:
                    act.wait_ge(shifted_h0, v)
                    for b in range(2):
                        last = go(h0[0:1, 2 * b, :], cls_sb[:], ACT.Copy)
                    last.then_inc(h0_ready, 1)
                if u == 6:
                    act.wait_ge(xn1_t, v)
                    go(xT1[:, 0:PAIR], A[:, 2, 0:PAIR], ACT.Copy).then_inc(xT1_ready, 1)
                if u in (6, 7):
                    n = 2 * (u - 6) + 1
                    act.wait_ge(qk_done[n], v)
                    for r in range(4):
                        last = go(k_sb[32 * r:32 * r + 32, n // 2, r, :],
                                  A[32 * r:32 * r + 32, (3 + n) % 4, 0:PAIR], ACT.Copy)
                    last.then_inc(qk_ready[n], 1)
                if u == 8:
                    act.wait_ge(v_done, v)
                    go(v_sb[:, :, :, 0:HD], A[0:T, 3, :].rearrange("p (j h d) -> p j h d", j=4, h=HEADS), ACT.Copy
                       ).then_inc(v_ready, 1)
                if 9 <= u < 17:
                    c = u - 9
                    exponentials(c, 1, halves)
                    act.wait_ge(pt_done[0][c], v)
                    go(probT[:, c % 2, 0], A[0:T, 2, 0:4 * T].rearrange("p (r q) -> p r q", r=4), ACT.Copy
                       ).then_inc(pt_ready[0][c], 1)
                if 8 <= u < 16:
                    exponentials(u - 8, 0, halves)
                if u == 23:
                    act.wait_ge(xn2_t, v)
                    go(xT2[:, 0:PAIR], A[:, 1, 0:PAIR], ACT.Copy).then_inc(xT2_ready, 1)
                if u == 26:
                    act.wait_ge(shifted_ready, v)
                    go(expl[:], shifted[:, :, 0:EXPERTS], ACT.Exp).then_inc(expl_ready, 1)
                if u == 4 and v_conv is not None:
                    for part in range(3):
                        patches(part, v_conv)

            def expert(i, n2):
                act.wait_ge(gate_done, n2)
                go(tanh[:, i % 2, :], gate_ps[:, i % 2, 0:PAIR], ACT.Tanh, scale=0.5).then_inc(tanh_done, 1)

            def take_shares(v, fillings):
                act.wait_ge(share_t, v)
                if fillings is not None:
                    for k in (ROUTED - 2, ROUTED - 1):
                        act.wait_ge(spread_in[k % SLOTS], fillings)
                go(share_sb[:], A[0:EXPERTS, 3, 0:PAIR], ACT.Copy, scale=0.5).then_inc(share_sb_ready, 1)

            def hand_over(v, units):
                act.wait_ge(up_done, units)
                act.wait_ge(xT2_ready, v)
                go(x_hi[:], xT2[:, 0:PAIR], ACT.Copy).then_inc(x_hi_ready, 1)

            def read_y(v):
                act.wait_ge(y_done, v)
                go(y_sb[:, 0:NTOK + 1], y_ps[:, 0:NTOK + 1], ACT.Copy).then_inc(y_half_read, 1)
                go(y_sb[:, NTOK + 1:PAIR], y_ps[:, NTOK + 1:PAIR], ACT.Copy).then_inc(y_read, 1)

            act.wait_ge(consts_in, 16 * 15)
            act.wait_ge(presets, 5)
            act.sem_inc(tanh_done, 1)
            for part in range(3):
                patches(part, 1)
            for u in range(UNITS):
                for at, n, hi in ((4, 0, gate_hi), (17, 1, up_hi)):
                    if u == at:
                        act.wait_ge(stage_in, 16 * (n + 1))
                        go(hi[:].rearrange("p u m -> p (u m)"), stage, ACT.Copy).then_inc(split_step, 1)
                attention(u, 1, 0, 2)
            take_shares(1, None)
            hand_over(1, 1)

            def experts_and_attention(base, v, v_next, halves, fillings, v_conv):
                for i in range(UNITS):
                    expert(i, base + (i + 2))
                    attention(i, v_next, halves, v_conv)
                take_shares(v_next, fillings)
                hand_over(v_next, base + (UNITS + 1))
                read_y(v)

            with act.Fori(0, PAIRS - 2) as p:
                experts_and_attention(act.snap(p * UNITS), act.snap(p + 1), act.snap(p + 2),
                                      act.snap(HALVES * (p + 1)), act.snap((p + 1) * FILLED), act.snap(p + 3))
            experts_and_attention((PAIRS - 2) * UNITS, PAIRS - 1, PAIRS, HALVES * (PAIRS - 1),
                                  (PAIRS - 1) * FILLED, None)
            for i in range(UNITS):
                expert(i, (PAIRS - 1) * UNITS + i + 2)
            read_y(PAIRS)

        @block.vector
        def _(dve):
            V = nc.vector

            def statistics(k, src, v):
                for j in range(4):
                    last = V.bn_stats(bn[:, k, j, :], src[:, j, :])
                last.then_inc(bn_done[k], 1)
                hold(dve, bn_done[k], v)
                for j in range(4):
                    last = V.bn_aggr(mv[:, k, j, :], bn[:, k, j, :])
                last.then_inc(var_ready[k], 1)

            def normalise(k, dst, src, v):
                dve.wait_ge(rstd_ready[k], v)
                for j in range(4):
                    last = V.tensor_scalar(dst[:, j, :], src[:, j, :], mv[:, k, j, 0:1], rstd[:, k, j:j + 1],
                                           ALU.subtract, ALU.mult)
                return last

            def attention(u, v, halves, route):
                tok = A[0:T, 1, :].rearrange("p (j d) -> p j d", j=4)
                if u == 0:
                    dve.wait_ge(raw_t, v)
                    statistics(0, tok, v)
                if u == 1:
                    normalise(0, xn, tok, v).then_inc(z_ready, 1)
                if u == 3:
                    dve.wait_ge(h0_ready, v)
                    statistics(1, h0, v)
                if u == 4:
                    normalise(1, xn, h0, v).then_inc(xn1_ready, 1)
                if u in (6, 7):
                    n = 2 * (u - 6)
                    dve.wait_ge(qk_done[n], v)
                    V.tensor_scalar(q_sb[:, n // 2, 0:PAIR], A[:, (3 + n) % 4, 0:PAIR], HD ** -0.5, None, ALU.mult
                                    ).then_inc(qk_ready[n], 1)
                if 8 <= u < 16:
                    c = u - 8
                    for h in range(2):
                        dve.wait_ge(score_halves, halves + (2 * c + h + 1))
                        V.tensor_reduce(negmax[:, c, 2 * h:2 * h + 2], SCORES[:, h], AX_X, ALU.max, negate=True
                                        ).then_inc(max_halves, 1)
                if 10 <= u < 18:
                    c = u - 10
                    b, g, half = combo(c)
                    j = 2 * b + half
                    dve.wait_ge(pv_done[c], v)
                    V.tensor_copy(heads[:, g, START[j]:START[j] + WIDTH[j]], A[:, 3, 0:WIDTH[j]]
                                  ).then_inc(pv_read[c], 1)
                if 9 <= u < 17:
                    c = u - 9
                    dve.wait_ge(pt_done[1][c], v)
                    V.tensor_copy(probT[:, c % 2, 1], A[0:T, 2, 0:4 * T].rearrange("p (r q) -> p r q", r=4)
                                  ).then_inc(pt_ready[1][c], 1)
                if u == 16:
                    dve.wait_ge(exp_halves, halves + HALVES)
                    V.reciprocal(rinv[:], sums[:]).then_inc(rinv_done, 1)
                if u == 17:
                    dve.wait_ge(rinv_done, v)
                    dve.wait_ge(out_free, v)
                    for g in range(2):
                        for j in range(4):
                            last = V.tensor_copy(rwide[g][:, j, :].rearrange("p (r d) -> p r d", r=4),
                                                 rinv[:, j, 4 * g:4 * g + 4].unsqueeze(2).to_broadcast([T, 4, 32]))
                    last.then_inc(rwide_ready, 1)
                if u == 18:
                    dve.wait_ge(rwide_t, v)
                    dve.wait_ge(pv_read[7], v)
                    for g in range(2):
                        last = V.tensor_tensor(heads[:, g, 0:PAIR], heads[:, g, 0:PAIR], A[:, g, 0:PAIR], ALU.mult)
                    last.then_inc(heads_ready, 1)
                if u == 19:
                    dve.wait_ge(proj_done, v)
                    dve.wait_ge(h0_biased, v)
                    dve.wait_ge(resid_copied, v)
                    V.tensor_tensor(h1[:].rearrange("p j d -> p (j d)"), A[0:T, 2, :],
                                    h0[:].rearrange("p j d -> p (j d)"), ALU.add).then_inc(h1_ready, 1)
                if u == 20:
                    dve.wait_ge(h1_ready, v)
                    statistics(2, h1, v)
                if u == 22:
                    normalise(2, xn, h1, v).then_inc(xn2_ready, 1)
                if u == 24:
                    dve.wait_ge(logits_done, v)
                    V.tensor_tensor(logit[:], A[0:T, 3, 0:4 * EXPERTS].rearrange("p (j e) -> p j e", j=4),
                                    brout_sb[:].unsqueeze(1).to_broadcast([T, 4, EXPERTS]),
                                    ALU.add).then_inc(route_step, 1)
                    dve.wait_ge(route_step, route + 1)
                    V.tensor_reduce(lmax[:], logit[:], AX_X, ALU.max).then_inc(route_step, 1)
                if u == 25:
                    dve.wait_ge(route_step, route + 2)
                    V.tensor_tensor(logit[:], logit[:], lmax[:].unsqueeze(2).to_broadcast([T, 4, EXPERTS]),
                                    ALU.subtract).then_inc(route_step, 1)
                    dve.wait_ge(route_step, route + 3)
                    V.tensor_scalar(shifted[:, :, 0:EXPERTS], logit[:], LOWEST, None, ALU.max
                                    ).then_inc(shifted_ready, 1)
                if u == 26:
                    hold(dve, shifted_ready, v)
                    for j in range(4):
                        last = V.max(top8[:, j, :], shifted[:, j, 0:EXPERTS])
                    last.then_inc(route_step, 1)
                    dve.wait_ge(route_step, route + 4)
                    V.tensor_copy(topr[:, :, 0:TOPK], top8[:, :, 0:TOPK]).then_inc(route_step, 1)
                if u == 27:
                    hold(dve, route_step, route + 5)
                    for j in range(4):
                        last = V.match_replace(marked[:, j, :], topr[:, j, :], shifted[:, j, :], CHOSEN)
                    last.then_inc(route_step, 1)
                if u == 28:
                    dve.wait_ge(route_step, route + 6)
                    V.tensor_scalar(chosen[:], marked[:, :, 0:EXPERTS], CHOSEN, None, ALU.is_equal
                                    ).then_inc(chosen_ready, 1)
                    dve.wait_ge(expl_ready, v)
                    V.tensor_reduce(zsum[:, 0, :], expl[:], AX_X, ALU.add).then_inc(route_step, 1)
                    dve.wait_ge(route_step, route + 7)
                    V.scalar_tensor_tensor(expc[:], marked[:, :, 0:EXPERTS], CHOSEN, expl[:], ALU.is_equal, ALU.mult
                                           ).then_inc(route_step, 1)
                if u == 29:
                    dve.wait_ge(route_step, route + 8)
                    V.tensor_reduce(zsum[:, 1, :], expc[:], AX_X, ALU.add).then_inc(route_step, 1)
                    dve.wait_ge(route_step, route + 9)
                    V.scalar_tensor_tensor(zsum[:, 2, :], zsum[:, 0, :], GATE_EPS, zsum[:, 1, :], ALU.mult, ALU.add
                                           ).then_inc(route_step, 1)
                    dve.wait_ge(route_step, route + 10)
                    V.reciprocal(rden[:], zsum[:, 2, :]).then_inc(rden_ready, 1)
                if u == 30:
                    dve.wait_ge(rank_done, v)
                    V.tensor_tensor(slot[:], A[0:T, 2, 0:4 * EXPERTS].rearrange("p (j e) -> p j e", j=4),
                                    counts[:].unsqueeze(1).to_broadcast([T, 4, EXPERTS]), ALU.add
                                    ).then_inc(route_step, 1)
                    dve.wait_ge(route_step, route + 11)
                    V.tensor_tensor(counts[:], A[0:T, 2, 4 * EXPERTS:5 * EXPERTS], counts[:], ALU.add)
                if u == 31:
                    V.scalar_tensor_tensor(kept, slot[:], CAPACITY, expc[:], ALU.is_lt, ALU.mult
                                           ).then_inc(route_step, 1)
                    dve.wait_ge(route_step, route + 12)
                    dve.wait_ge(rden_ready, v)
                    V.tensor_tensor(share_tok[:, :, 0:EXPERTS], kept,
                                    rden[:].unsqueeze(2).to_broadcast([T, 4, EXPERTS]), ALU.mult
                                    ).then_inc(share_tok_ready, 1)

            def expert(i, n2, fillings):
                h = hidden[:, i % 3, :]
                dve.wait_ge(tanh_done, n2)
                V.scalar_tensor_tensor(h, tanh[:, i % 2, :], 1.0, gate_ps[:, i % 2, 0:PAIR], ALU.add, ALU.mult
                                       ).then_inc(silu_done, 1)
                dve.wait_ge(silu_done, n2)
                dve.wait_ge(up_done, n2)
                V.tensor_tensor(h, h, up_ps[:, 0:PAIR], ALU.mult).then_inc(gated_done, 1)
                if i in BY_POOL:
                    return
                dve.wait_ge(gated_done, n2)
                if i < ROUTED:
                    dve.wait_ge(spread_in[i % SLOTS], fillings + 32 * (i // SLOTS + 1))
                    V.tensor_tensor(h, h, spread[:, i % SLOTS, :], ALU.mult).then_inc(hidden_done, 1)
                else:
                    dve.wait_ge(hidden_done, n2 - 1)
                    V.tensor_scalar(h, h, 0.25, None, ALU.mult).then_inc(hidden_done, 1)

            def add_output(v):
                dve.wait_ge(y_t, v)
                dve.wait_ge(resid_copied, v + 1)
                dve.wait_ge(out_free, v + 1)
                V.tensor_tensor(out_sb[:].rearrange("p j d -> p (j d)"), A[0:T, 2, :],
                                resid[:].rearrange("p j d -> p (j d)"), ALU.add).then_inc(out_added, 1)

            for t in (raw[:], pad_y[:], pad_x[:], xT1[:], q_sb[:], k_sb[:], v_sb[:], prob[:], heads[:], xT2[:], counts[:],
                      share_tok[:]):
                V.memset(t, 0.0)
            V.memset(topr[:], FILLER)
            V.memset(shifted[:], FILLER)
            V.memset(half_neg[:], -0.5).then_inc(presets, 4)
            dve.sem_inc(silu_done, 1)
            dve.sem_inc(gated_done, 1)
            dve.sem_inc(hidden_done, 1)
            dve.sem_inc(gate_done, 1)
            dve.sem_inc(up_done, 1)
            dve.sem_inc(out_added, CREDITS_Y)
            dve.sem_inc(out_free, CREDITS_Y)
            dve.sem_inc(resid_copied, 1)
            dve.wait_ge(consts_in, 16 * 15)
            V.tensor_copy(before_sb[:], before_f).then_inc(presets, 1)
            dve.wait_ge(presets, 5)
            for u in range(UNITS):
                attention(u, 1, 0, 0)

            def experts_and_attention(base, fillings, v, v_next, halves, route):
                for i in range(UNITS):
                    expert(i, base + (i + 2), fillings)
                    attention(i, v_next, halves, route)
                add_output(v)

            with dve.Fori(0, PAIRS - 2) as p:
                experts_and_attention(dve.snap(p * UNITS), dve.snap(p * FILLED), dve.snap(p + 1), dve.snap(p + 2),
                                      dve.snap(HALVES * (p + 1)), dve.snap(ROUTE_STEPS * (p + 1)))
            experts_and_attention((PAIRS - 2) * UNITS, (PAIRS - 2) * FILLED, PAIRS - 1, PAIRS,
                                  HALVES * (PAIRS - 1), ROUTE_STEPS * (PAIRS - 1))
            for i in range(UNITS):
                expert(i, (PAIRS - 1) * UNITS + i + 2, (PAIRS - 1) * FILLED)
            add_output(PAIRS)

        @block.gpsimd
        def _(pool):
            G = nc.gpsimd

            def root(k, v):
                hold(pool, var_ready[k], v)
                G.tensor_scalar(var_eps[:, k, :], mv[:, k, :, 1], EPS, None, ALU.add).then_inc(eps_added[k], 1)
                pool.wait_ge(eps_added[k], v)
                G.tensor_tensor(rstd[:, k, :], var_eps[:, k, :], half_neg[:], ALU.pow).then_inc(rstd_ready[k], 1)

            def neighbours(v):
                pool.wait_ge(conv_read, v)
                for pad, sem_, places in ((pad_y, raw_step, ((64, 2, 1), (96, 0, 1))),
                                          (pad_x, raw_ready, ((64, 1, 2), (96, 1, 0)))):
                    for at, dy, dx in places:
                        dst = raw[at:at + 32, 0:PAIR].rearrange("p (b n) -> p b n", b=2)[:, :, 1:NTOK].rearrange(
                            "p b (t x) -> p b t x", x=GRID)
                        last = G.tensor_tensor(dst, dst, pad[at:at + 32, :, dy:dy + GRID, dx:dx + GRID], ALU.add)
                    last.then_inc(sem_, 1)
                    pool.wait_ge(sem_, v)

            def attention(u, v, v_conv):
                if u == 0:
                    root(0, v)
                if u == 1:
                    pool.wait_ge(z_ready, v)
                    G.tensor_tensor(xn[:], xn[:], lng_sb[:].unsqueeze(1).to_broadcast([T, 4, 128]), ALU.mult
                                    ).then_inc(scaled, 1)
                    pool.wait_ge(scaled, v)
                    G.tensor_tensor(h0[:], xn[:], lnb_sb[:].unsqueeze(1).to_broadcast([T, 4, 128]), ALU.add).then_inc(shifted_h0, 1)
                if u == 3:
                    root(1, v)
                if u == 4:
                    pool.wait_ge(xn1_ready, v)
                    G.tensor_tensor(h0[:], h0[:], bproj_sb[:].unsqueeze(1).to_broadcast([T, 4, 128]), ALU.add).then_inc(h0_biased, 1)
                if u == 20:
                    root(2, v)
                if u == 5 and v_conv is not None:
                    pool.wait_ge(h0_biased, v)
                    neighbours(v_conv)

            def expert(i, n2, fillings):
                if i in BY_POOL:
                    pool.wait_ge(gated_done, n2)
                    pool.wait_ge(spread_in[i % SLOTS], fillings + 32 * (i // SLOTS + 1))
                    G.tensor_tensor(hidden[:, i % 3, :], hidden[:, i % 3, :], spread[:, i % SLOTS, :], ALU.mult
                                    ).then_inc(hidden_done, 1)

            def hand_over(v):
                pool.wait_ge(x_hi_ready, v)
                G.tensor_tensor(x_lo[:], xT2[:, 0:PAIR], x_hi[:].bitcast(F32), ALU.subtract).then_inc(x_lo_ready, 1)
                pool.wait_ge(h1_ready, v)
                hold(pool, out_added, v + 1)
                G.tensor_copy(resid[:], h1[:]).then_inc(resid_copied, 1)

            pool.wait_ge(consts_in, 16 * 15)
            pool.wait_ge(presets, 5)
            neighbours(1)
            for u in range(UNITS):
                attention(u, 1, 2)
                for at, n, hi, lo in ((6, 0, gate_hi, gate_lo), (20, 1, up_hi, up_lo)):
                    if u == at:
                        pool.wait_ge(split_step, 2 * n + 1)
                        G.tensor_tensor(lo[:].rearrange("p u m -> p (u m)"), stage,
                                        hi[:].rearrange("p u m -> p (u m)").bitcast(F32), ALU.subtract
                                        ).then_inc(split_step, 1)
            hand_over(1)

            def experts_and_attention(base, fillings, v_next, v_conv):
                for i in range(UNITS):
                    expert(i, base + (i + 2), fillings)
                    attention(i, v_next, v_conv)
                hand_over(v_next)

            with pool.Fori(0, PAIRS - 2) as p:
                experts_and_attention(pool.snap(p * UNITS), pool.snap(p * FILLED),
                                      pool.snap(p + 2), pool.snap(p + 3))
            experts_and_attention((PAIRS - 2) * UNITS, (PAIRS - 2) * FILLED, PAIRS, None)
            for i in range(UNITS):
                expert(i, (PAIRS - 1) * UNITS + i + 2, (PAIRS - 1) * FILLED)


def kernel(**inputs):
    import numpy as np
    import concourse.bacc as bacc
    from concourse.bass_utils import run_bass_kernel_spmd as run

    a = {k: np.asarray(v) for k, v in inputs.items()}
    f4 = np.float32
    P = PS

    main = a["L0_tok_W_main"].reshape(64, 3, P, 2, HP).transpose(3, 1, 2, 4, 0)
    sy = a["L0_tok_W_sy"].reshape(16, 3, P, 2, HP).transpose(3, 1, 2, 4, 0)
    sx = a["L0_tok_W_sx"].reshape(16, 3, P, 2, HP).transpose(3, 1, 2, 4, 0)
    conv = np.zeros((2, 3, P, HP, 128), f4)
    conv[..., 0:64] = main
    conv[:, :, HP:, :, 64:80] = sy[:, :, :HP]
    conv[1, ..., 80:96] = sx[0]
    conv[:, :, :HP, :, 96:112] = sy[:, :, HP:]
    conv[0, ..., 112:128] = sx[1]
    bm, bx, by = a["L0_tok_b_main"], a["L0_tok_b_sx"], a["L0_tok_b_sy"]
    conv_b = np.concatenate([bm, by, bx, by, bx]).reshape(128, 1)
    masks = np.zeros((4, 2, 16, 2), f4)
    masks[:, 0, :, 0] = 1
    masks[:, 1, :, 1] = 1
    perm = np.zeros((128, 128), f4)
    order = np.concatenate([np.arange(64), np.arange(96, 112), np.arange(64, 80), np.arange(112, 128),
                            np.arange(80, 96)])
    perm[np.arange(128), order] = 1

    qkv = a["L0_attn_w_qkv"].reshape(3, 2, 4, HD, D)
    w_qk = np.zeros((D, 2, 2, 4, 32), f4)
    w_qk[..., 0:HD] = qkv[0:2].transpose(4, 1, 0, 2, 3)
    w_p = np.zeros((2, 4, 32, D), f4)
    w_p[:, :, 0:HD, :] = a["L0_attn_w_proj"].T.reshape(2, 4, HD, D)

    def by_feature(routed, shared):
        return np.concatenate([routed.reshape(-1, D), shared.reshape(-1, D)]).T

    down = np.concatenate([a["L0_ffn_w_down"], a["L0_ffn_shared_w_down"]]).transpose(0, 2, 1)
    before = np.ones((T, 2, T), f4)
    before[:, 0, :] = np.triu(np.ones((T, T), f4), 1)

    arrays = {
        "x": a["x"], "conv_w": conv.reshape(96, HP * 128), "conv_b": conv_b, "masks": masks.reshape(128, 2),
        "perm": perm, "ident": np.eye(128, dtype=f4), "cls_tok": a["cls_tok"].reshape(1, D),
        "ln_g": np.broadcast_to(a["L0_tok_ln_g"], (T, D)), "ln_b": np.broadcast_to(a["L0_tok_ln_b"], (T, D)),
        "w_qk": w_qk.reshape(D, 512), "w_v": qkv[2].reshape(D, D).T,
        "w_p": w_p.reshape(2, 128, D).transpose(1, 0, 2).reshape(128, 256),
        "b_proj": np.broadcast_to(a["L0_attn_b_proj"], (T, D)),
        "w_r": a["L0_ffn_router_w"].T, "b_r": np.broadcast_to(a["L0_ffn_bias"], (T, EXPERTS)),
        "w_gate": by_feature(a["L0_ffn_w_gate"], a["L0_ffn_shared_w_gate"]),
        "w_up": by_feature(a["L0_ffn_w_up"], a["L0_ffn_shared_w_up"]),
        "w_down": down.reshape(UNITS, 128, D).transpose(1, 0, 2).reshape(128, UNITS * D),
        "before": before.reshape(T, 2 * T),
    }
    arrays = {k: np.ascontiguousarray(v) for k, v in arrays.items()}
    nc = bacc.Bacc("TRN2", target_bir_lowering=False, num_devices=1)
    args = [nc.dram_tensor(f"in_{k}", v.shape, mybir.dt.from_np(v.dtype), kind="ExternalInput").ap()
            for k, v in arrays.items()]
    shape = (a["x"].shape[0], NTOK, D)
    args.append(nc.dram_tensor("out_0", shape, F32, kind="ExternalOutput").ap())
    vit_layer(nc, **dict(zip(list(arrays) + ["out"], args)))
    r = run(nc, [{f"in_{k}": v for k, v in arrays.items()}], core_ids=[0])
    return r.results[0]["out_0"]
```
